# Optimizing a Trainium2 kernel written in Bass

```python
import numpy as np
import jax
import jax.numpy as jnp

def _softmax(x, axis=-1):
    return jax.nn.softmax(x, axis=axis)

def _gelu(x):
    return jax.nn.gelu(x, approximate=True)

def _silu(x):
    return jax.nn.silu(x)

def _sigmoid(x):
    return jax.nn.sigmoid(x)

def _layernorm(x, axis=-1, eps=1e-05):
    m = jnp.mean(x, axis=axis, keepdims=True)
    v = jnp.var(x, axis=axis, keepdims=True)
    return (x - m) / jnp.sqrt(v + eps)

def _scatter_add(tgt, idx, src, axis=0):
    return tgt.at[idx].add(src)

def _segment_sum(src, seg, n):
    return jax.ops.segment_sum(src, seg, n)
kernel_name = 'mk_seq_postln_d1_jaxref_r4_0ffbc5'

def setup_inputs(seed: int=0):
    np.random.seed(seed)
    _w = jnp.asarray

    def _L0_attn_setup():
        import math
        import jax, jax.numpy as jnp
        import numpy as np
        NUM_HEAD = 16
        EMB = 512
        HEAD_DIM = EMB // NUM_HEAD
        B, T = (2, 512)

        def get_slopes(n):
            start = 2 ** (-2 ** (-(math.log2(n) - 3)))
            return np.array([start * start ** i for i in range(n)], dtype=np.float32)
        key = jax.random.key(seed)
        ks = jax.random.split(key, 5)
        x = jax.random.normal(ks[0], (B, T, EMB), jnp.float32)

        def w(k, scale=0.02):
            return jax.random.normal(k, (EMB, EMB), jnp.float32) * scale
        return {'x': x, 'Wq': w(ks[1]), 'bq': jnp.zeros((EMB,), jnp.float32), 'Wk': w(ks[2]), 'bk': jnp.zeros((EMB,), jnp.float32), 'Wv': w(ks[3]), 'bv': jnp.zeros((EMB,), jnp.float32), 'Wo': w(ks[4], scale=0.02 / math.sqrt(24)), 'bo': jnp.zeros((EMB,), jnp.float32)}
    _L0_attn_in = _L0_attn_setup()

    def _L0_ffn_setup():
        import jax, jax.numpy as jnp
        import numpy as np
        D_MODEL = 512
        D_FF = 2048
        N_EXPERTS = 4
        B, S = (2, 512)
        key = jax.random.key(seed)
        ks = jax.random.split(key, 6)
        scale = 0.02
        return {'hidden_states': jax.random.normal(ks[0], (B, S, D_MODEL), dtype=jnp.float32), 'Wr': jax.random.normal(ks[1], (D_MODEL, N_EXPERTS), dtype=jnp.float32) * scale, 'br': jnp.zeros((N_EXPERTS,), dtype=jnp.float32), 'Wg': jax.random.normal(ks[2], (N_EXPERTS, D_MODEL, D_FF), dtype=jnp.float32) * scale, 'Wu': jax.random.normal(ks[3], (N_EXPERTS, D_MODEL, D_FF), dtype=jnp.float32) * scale, 'Wd': jax.random.normal(ks[4], (N_EXPERTS, D_FF, D_MODEL), dtype=jnp.float32) * scale}
    _L0_ffn_in = _L0_ffn_setup()
    _d = {'L0_attn_x': _L0_attn_in['x'], 'L0_attn_Wq': _L0_attn_in['Wq'], 'L0_attn_bq': _L0_attn_in['bq'], 'L0_attn_Wk': _L0_attn_in['Wk'], 'L0_attn_bk': _L0_attn_in['bk'], 'L0_attn_Wv': _L0_attn_in['Wv'], 'L0_attn_bv': _L0_attn_in['bv'], 'L0_attn_Wo': _L0_attn_in['Wo'], 'L0_attn_bo': _L0_attn_in['bo'], 'L0_ffn_Wr': _L0_ffn_in['Wr'], 'L0_ffn_br': _L0_ffn_in['br'], 'L0_ffn_Wg': _L0_ffn_in['Wg'], 'L0_ffn_Wu': _L0_ffn_in['Wu'], 'L0_ffn_Wd': _L0_ffn_in['Wd']}
    _x0 = _d['L0_attn_x']
    _d['L0_attn_x'] = jax.random.normal(jax.random.fold_in(jax.random.key(seed), 1), (4, 512, 512), dtype=_x0.dtype)
    del _x0
    return _d

def reference(L0_attn_x, L0_attn_Wq, L0_attn_bq, L0_attn_Wk, L0_attn_bk, L0_attn_Wv, L0_attn_bv, L0_attn_Wo, L0_attn_bo, L0_ffn_Wr, L0_ffn_br, L0_ffn_Wg, L0_ffn_Wu, L0_ffn_Wd):

    def _L0_attn_ref(x, Wq, bq, Wk, bk, Wv, bv, Wo, bo):
        import math
        import jax, jax.numpy as jnp
        import numpy as np
        NUM_HEAD = 16
        EMB = 512
        HEAD_DIM = EMB // NUM_HEAD
        B, T = (2, 512)

        def get_slopes(n):
            start = 2 ** (-2 ** (-(math.log2(n) - 3)))
            return np.array([start * start ** i for i in range(n)], dtype=np.float32)
        Bx, Tx, C = x.shape
        slopes = jnp.asarray(get_slopes(NUM_HEAD))

        def split_heads(y):
            return y.reshape(Bx, Tx, NUM_HEAD, HEAD_DIM).transpose(0, 2, 1, 3)
        q = split_heads(x @ Wq + bq)
        k = split_heads(x @ Wk + bk)
        v = split_heads(x @ Wv + bv)
        attn = jnp.einsum('bhqd,bhkd->bhqk', q, k) / jnp.sqrt(jnp.float32(HEAD_DIM))
        alibi = -slopes[:, None, None] * (Tx - 1 - jnp.arange(Tx, dtype=jnp.float32))[None, None, :]
        attn = attn + alibi
        causal = jnp.tril(jnp.ones((Tx, Tx), dtype=bool))[None, None]
        attn = jnp.where(causal, attn, jnp.finfo(jnp.float32).min)
        p = jax.nn.softmax(attn, axis=-1)
        out = jnp.einsum('bhqk,bhkd->bhqd', p, v).transpose(0, 2, 1, 3).reshape(Bx, Tx, C)
        return out @ Wo + bo

    def _L0_ffn_ref(hidden_states, Wr, br, Wg, Wu, Wd):
        import jax, jax.numpy as jnp
        import numpy as np
        D_MODEL = 512
        D_FF = 2048
        N_EXPERTS = 4
        B, S = (2, 512)
        b, s, d = hidden_states.shape
        x = hidden_states.reshape(-1, d)
        logits = x @ Wr + br
        probs = jax.nn.softmax(logits, axis=-1)
        top_w, top_idx = jax.lax.top_k(probs, 1)
        g = jnp.einsum('td,edf->tef', x, Wg)
        u = jnp.einsum('td,edf->tef', x, Wu)
        h = jax.nn.silu(g) * u
        y = jnp.einsum('tef,efd->ted', h, Wd)
        sel = jnp.take_along_axis(y, top_idx[:, :, None], axis=1)[:, 0]
        out = sel * top_w
        return out.reshape(b, s, d)
    x = L0_attn_x
    x = _layernorm(x + _L0_attn_ref(x, L0_attn_Wq, L0_attn_bq, L0_attn_Wk, L0_attn_bk, L0_attn_Wv, L0_attn_bv, L0_attn_Wo, L0_attn_bo), axis=-1)
    x = _layernorm(x + _L0_ffn_ref(x, L0_ffn_Wr, L0_ffn_br, L0_ffn_Wg, L0_ffn_Wu, L0_ffn_Wd), axis=-1)
    return x

_drawn_inputs = setup_inputs


def setup_inputs(seed=0):
    import zlib

    import numpy as np

    out = dict(_drawn_inputs(seed))
    spreads = {'L0_attn_bq': (0.0, 0.8),
     'L0_attn_bk': (0.0, 0.8),
     'L0_attn_bv': (0.0, 0.8),
     'L0_attn_bo': (0.0, 0.1),
     'L0_ffn_br': (0.0, 0.394)}
    factors = {'L0_attn_Wq': 8.0, 'L0_attn_Wk': 8.0, 'L0_attn_Wv': 4.601, 'L0_attn_Wo': 3.733}
    for name, (base, spread) in spreads.items():
        noise = np.random.default_rng([zlib.crc32(name.encode()), seed]).standard_normal(out[name].shape)
        drawn = base * np.exp(spread * noise) if base else spread * noise
        out[name] = jnp.asarray(drawn.astype(out[name].dtype))
    for name, factor in factors.items():
        out[name] = (out[name] * factor).astype(out[name].dtype)
    return out
```

```python
import math
from collections import deque
from contextlib import ExitStack

import numpy as np

import concourse.bass as bass
from concourse import mybir

F32 = mybir.dt.float32
F32R = mybir.dt.float32r
I32 = mybir.dt.int32
U32 = mybir.dt.uint32
ALU = mybir.AluOpType
ACT = mybir.ActivationFunctionType
AX_X = mybir.AxisListType.X

P = 128
NB, SEQ, D = 4, 512, 512
NH = 16
HD = D // NH
GH = P // HD
KT = D // P
QT = SEQ // P
NG = NB * (NH // GH)
GPB = NH // GH
NT = NB * QT
NE, FF = 4, 2048
NS = NT + NE - 1
NC = FF // P
ROW = D + 4
TRASH = 4095
EPS = 1e-5
MASKED = -1e30

C_FULL, C_SLOT, C_TOKEN, C_QSCALE = 0, NT, NT + NS, NT + NS + NT
N_SMALL = C_QSCALE + KT


class Signal:

    def __init__(self, ctx, nc, name):
        self.sem = ctx.enter_context(nc.semaphore(name))
        self.value = 0


class Lane:

    def __init__(self):
        self.steps = []
        self.waited = {}

    def wait(self, *tickets):
        for signal, value in tickets:
            if self.waited.get(signal, 0) < value:
                self.waited[signal] = value
                self.steps.append(lambda eng, s=signal.sem, v=value: eng.wait_ge(s, v))

    def run(self, make, signal=None, by=1):
        if signal is None:
            self.steps.append(make)
            return None
        self.steps.append(lambda eng: make(eng).then_inc(signal.sem, by))
        signal.value += by
        return (signal, signal.value)

    def emit(self, eng):
        for step in self.steps:
            step(eng)


class Map:

    def __init__(self, nc, at):
        self.nc, self.at = nc, (at + 31) // 32 * 32

    def put(self, name, shape, dtype):
        t = self.nc.alloc_sbuf_tensor_at(name, shape, dtype, offset=self.at)
        self.at += (4 * int(np.prod(shape[1:])) + 31) // 32 * 32
        return t


def slopes():
    start = 2 ** (-2 ** (-(math.log2(NH) - 3)))
    return [float(np.float32(start * start ** i)) for i in range(NH)]


def build(nc, x, Wq, bq, Wk, bk, Wv, bv, Wo, bo, Wr, br, Wg, Wu, Wd,
          c_ident, c_dist, c_before, c_small, c_qscale, out):
    SLOPE = slopes()
    xs_dram = nc.dram_tensor("xs_scratch", (NS * P, ROW), F32, kind="Internal").ap()
    x_rows = x.rearrange("b (t p) d -> b p t d", p=P)
    out_rows = out.rearrange("b t d -> (b t) d")
    xs_rows = xs_dram.rearrange("(s p) d -> p s d", p=P)

    with ExitStack() as ctx:
        ctx.enter_context(nc.allow_non_contiguous_dma(reason="small vectors laid across partitions"))

        def signal(name):
            return Signal(ctx, nc, name)

        banks = [ctx.enter_context(nc.psum_tensor(f"bank{i}", [P, 512], F32)) for i in range(8)]
        pe, act, dve, pool, sp = (Lane() for _ in range(5))

        base = nc._sbuf_addr_for_side("left")
        keep = Map(nc, base)
        ident = keep.put("ident", [P, P], F32)
        small = keep.put("small", [P, N_SMALL], F32)
        logits = keep.put("logits", [P, NT, NE], F32)
        slot_expert = keep.put("slot_expert", [P, NS], I32)
        position = keep.put("position", [P, NT], I32)
        meta = keep.put("meta", [P, NS, 4], F32)
        token = keep.put("token", [P, NS], I32)
        stats = keep.put("stats", [P, 2, 6], F32)
        mv = keep.put("mv", [P, 2, 2], F32)
        rstd = keep.put("rstd", [P, 2, 2], F32)
        mhalf = keep.put("mhalf", [P, 1], F32)

        x1_map = Map(nc, keep.at)
        x1 = x1_map.put("x1", [P, NT, ROW], F32)
        w_raw = Map(nc, keep.at).put("w_raw", [P, 4, KT, D], F32)

        p1 = Map(nc, x1_map.at)
        WK, WQ, WV, WO = range(4)
        w_hi = p1.put("w_hi", [P, 4, KT, D], F32R)
        w_lo = p1.put("w_lo", [P, 4, KT, D], F32R)
        dist = p1.put("dist", [P, SEQ], F32)
        x_tok = p1.put("x_tok", [P, 2, QT, D], F32)
        xT_hi = p1.put("xT_hi", [P, KT, SEQ], F32R)
        xT_lo = p1.put("xT_lo", [P, KT, SEQ], F32R)
        qk_hi = p1.put("qk_hi", [P, 2, 2, SEQ], F32R)
        qk_lo = p1.put("qk_lo", [P, 2, 2, SEQ], F32R)
        vT = p1.put("vT", [P, SEQ], F32)
        v = p1.put("v", [P, 2, QT, GH, 2 * HD], F32R)
        route = Map(nc, p1.at).put("route", [P, 12, NT, NE], F32)
        scores = p1.put("scores", [P, 2, SEQ], F32)
        probs = p1.put("probs", [P, 2, SEQ], F32)
        pT_hi = p1.put("pT_hi", [P, 2, SEQ], F32R)
        pT_lo = p1.put("pT_lo", [P, 2, SEQ], F32R)
        o_tok = p1.put("o_tok", [P, 2, QT, D], F32)
        oT_hi = p1.put("oT_hi", [P, KT, P], F32R)
        oT_lo = p1.put("oT_lo", [P, KT, P], F32R)
        res = p1.put("res", [P, D], F32)
        x1T = p1.put("x1T", [P, KT, P], F32)
        bo_row = p1.put("bo_row", [P, D], F32)
        pv_hi = p1.put("pv_hi", [P, 2, GH, HD], F32)
        pv_sum = p1.put("pv_sum", [P, 2, GH, HD], F32)
        bias_col = p1.put("bias_col", [P, 3, GPB], F32)
        wr = p1.put("wr", [P, KT, NE], F32)
        br_row = p1.put("br_row", [P, NE], F32)
        neg_max = p1.put("neg_max", [P, 4], F32)
        row_sum = p1.put("row_sum", [P, 2, GH], F32)
        row_inv = p1.put("row_inv", [P, 2, GH], F32)
        qscale = p1.put("qscale", [P, D], F32)
        before = p1.put("before", [P, P], F32)
        ones = p1.put("ones", [P, P], F32)
        filler_row = p1.put("filler_row", [P, ROW], F32)
        assert p1.at <= nc._sbuf_addr_for_side("right"), p1.at

        s_x = [signal(f"x_loaded{i}") for i in range(2)]
        s_w = [signal(f"w_loaded{i}") for i in range(4)]
        s_const, s_const2 = signal("constants_loaded"), signal("late_constants_loaded")
        s_fill = signal("scratch_prefilled")
        s_pool = signal("pool_setup")
        s_whi, s_wlo = signal("w_hi_done"), signal("w_lo_done")
        s_scores, s_biased, s_exp = signal("scores_done"), signal("biased_done"), signal("exp_done")
        s_pT, s_pThi, s_pTlo = signal("pT_done"), signal("pT_hi_done"), signal("pT_lo_done")
        s_pv, s_pvhi, s_pvsum, s_o = signal("pv_done"), signal("pv_hi_copied"), signal("pv_summed"), signal("o_done")
        s_inv = signal("row_inverse_done")
        s_side = signal("side_products_done")
        s_side_act, s_side_dve, s_side_pool = signal("side_act"), signal("side_dve"), signal("side_pool")
        s_route = signal("route_dve")

        T = {}

        def load(dst, src, sig, lane=sp):
            return lane.run(lambda e: e.dma_start(dst, src), sig, 16)

        def load_x(b):
            return load(x_tok[:, b % 2, :, :], x_rows[b], s_x[b % 2])

        T["x", 0] = load_x(0)
        for t, src in ((ident[:, :], c_ident), (small[:, :], c_small)):
            load(t, src, s_const)
        for n, vec in enumerate((bk, bq, bv)):
            load(bias_col[:, n, :], vec.rearrange("(m p) -> p m", p=P), s_const)
        T["const"] = load(qscale[:, :], c_qscale, s_const)
        for n, W in ((WK, Wk), (WQ, Wq), (WV, Wv), (WO, Wo)):
            T["w", n] = load(w_raw[:, n, :, :], W.rearrange("(k p) n -> p k n", p=P), s_w[n])
            if n == WK:
                load(dist[:, :], c_dist, s_const2)
                load(before[:, :], c_before, s_const2)
                load(bo_row[:, :], bo.partition_broadcast(P), s_const2)
                load(br_row[:, :], br.partition_broadcast(P), s_const2)
                T["const2"] = load(wr[:, :, :], Wr.rearrange("(k p) e -> p k e", p=P), s_const2)
        T["x", 1] = load_x(1)

        pool.run(lambda e: e.memset(mhalf[:, :], -0.5), s_pool)
        pool.run(lambda e: e.memset(ones[:, :], 1.0), s_pool)
        T["zero"] = pool.run(lambda e: e.memset(filler_row[:, :], 0.0), s_pool)
        pool.wait(T["zero"])
        T["fill"] = pool.run(lambda e: e.memset(filler_row[:, D + 1:D + 2], float(TRASH)), s_pool)
        pool.wait(T["const2"])
        T["bq"] = pool.run(lambda e: e.tensor_tensor(bias_col[:, 1, :], bias_col[:, 1, :],
                                                     small[:, C_QSCALE:C_QSCALE + KT], ALU.mult), s_pool)
        pool.wait(T["w", WQ])
        for k in range(KT):
            T["wq"] = pool.run(lambda e, k=k: e.tensor_tensor(w_raw[:, WQ, k, :], w_raw[:, WQ, k, :],
                                                              qscale[:, :], ALU.mult), s_pool)
        sp.wait(T["fill"])
        for s in range(NS):
            T["scratch"] = load(xs_rows[:, s, :], filler_row[:, :], s_fill)

        def split_weight(n, hi_lane, lo_lane, need):
            hi_lane.wait(need)
            if hi_lane is act:
                T["whi", n] = act.run(lambda e: e.activation(w_hi[:, n, :, :], w_raw[:, n, :, :], ACT.Copy), s_whi)
            else:
                T["whi", n] = pool.run(lambda e: e.tensor_copy(w_hi[:, n, :, :], w_raw[:, n, :, :]), s_pool)
            lo_lane.wait(T["whi", n], need)
            sig = s_wlo if lo_lane is dve else s_pool
            T["wlo", n] = lo_lane.run(lambda e: e.tensor_tensor(
                w_lo[:, n, :, :], w_raw[:, n, :, :], w_hi[:, n, :, :].bitcast(F32), ALU.subtract), sig)

        side_banks = banks[6:8]
        side = {"n": 0, "free": [[], []], "job": None, "left": [], "bank": 0, "after": [], "later": deque()}
        queue = deque()

        def flush():
            for job, bank, done in side["after"]:
                side["free"][bank] = job["read"](side_banks[bank], done)
                side["later"].extend(job.get("later", []))
            side["after"] = []

        def flush_later(n=None):
            while side["later"] and (n is None or n > 0):
                side["later"].popleft()()
                n = None if n is None else n - 1

        def ticket(*key):
            key = key if len(key) > 1 else key[0]
            if key not in T:
                flush()
            if key not in T:
                flush_later()
            return T[key]

        def side_work(budget):
            while budget > 0 and (side["left"] or queue):
                if not side["left"]:
                    job = queue.popleft()
                    bank = side["n"] % 2
                    side["n"] += 1
                    if any(b == bank for _, b, _ in side["after"]):
                        flush()
                    pe.wait(*side["free"][bank])
                    pe.wait(*[ticket(*k) for k in job["need"]])
                    side.update(job=job, bank=bank, left=list(job["matmuls"]))
                cost, make = side["left"].pop(0)
                bank = side["bank"]
                last = not side["left"]
                done = pe.run(lambda e, m=make, t=side_banks[bank]: m(e, t), s_side if last else None)
                budget -= cost
                if last:
                    T[side["job"]["name"]] = done
                    side["after"].append((side["job"], bank, done))

        def queued_cost():
            return sum(c for c, _ in side["left"]) + sum(c for j in queue for c, _ in j["matmuls"])

        def transposes(src):
            return [(53, lambda e, t, j=j: e.transpose(t[:, j * P:(j + 1) * P], src(j), ident[:, :]))
                    for j in range(4)]

        def hi_lo_products(st_hi, st_lo, mv_hi, mv_lo, ns):
            steps = [(a, b, k) for k in range(KT) for a, b in ((st_hi, mv_hi), (st_lo, mv_hi), (st_hi, mv_lo))]
            return [(ns, lambda e, t, a=a, b=b, k=k, n=n: e.matmul(t[:, :], a(k), b(k), start=(n == 0),
                                                                   stop=(n == len(steps) - 1)))
                    for n, (a, b, k) in enumerate(steps)]

        def split_read(hi, lo, key, hi_wait, lo_wait):
            def read(bank, done):
                act.wait(done, *hi_wait())
                T[key + ("hi",)] = a = act.run(lambda e: e.activation(hi, bank[:, :], ACT.Copy), s_side_act)
                dve.wait(a, *lo_wait())
                T[key + ("lo",)] = b = dve.run(lambda e: e.tensor_tensor(lo, bank[:, :], hi.bitcast(F32),
                                                                         ALU.subtract), s_side_dve)
                return [a, b]
            return read

        def xT_job(b, k):
            free = (lambda: [T["VT", b * GPB - 1]]) if b else (lambda: [])
            return {"name": ("xT", b, k), "need": [("x", b), ("const",)],
                    "matmuls": transposes(lambda j: x_tok[:, b % 2, j, k * P:(k + 1) * P]),
                    "read": split_read(xT_hi[:, k, :], xT_lo[:, k, :], ("xT", b, k), free, free)}

        def project_job(kind, g):
            b, m = divmod(g, GPB)
            n = {"K": WK, "Q": WQ, "VT": WV}[kind]
            cols = slice(m * P, (m + 1) * P)
            bias = bias_col[:, n, m:m + 1]

            def read(bank, done):
                if kind == "VT":
                    act.wait(done, *([T["V", g - 1]] if g else []))
                    T["vT", g] = a = act.run(lambda e: e.activation(vT[:, :], bank[:, :], ACT.Identity, bias=bias),
                                             s_side_act)
                    return [a]
                hi, lo = qk_hi[:, g % 2, n, :], qk_lo[:, g % 2, n, :]
                free = [T["scores", g - 2]] if g >= 2 else []
                act.wait(done, *free)
                a = act.run(lambda e: e.activation(hi, bank[:, :], ACT.Identity, bias=bias), s_side_act)
                dve.wait(a, *free)
                T[kind, g, "lo"] = d = dve.run(lambda e: e.scalar_tensor_tensor(
                    lo, bank[:, :], bias, hi.bitcast(F32), ALU.add, ALU.subtract), s_side_dve)
                return [a, d]

            return {"name": (kind, g),
                    "need": [("whi", n), ("wlo", n), ("bq",)] + [("xT", b, k, p) for k in range(KT) for p in ("hi", "lo")],
                    "matmuls": hi_lo_products(lambda k: w_hi[:, n, k, cols], lambda k: w_lo[:, n, k, cols],
                                              lambda k: xT_hi[:, k, :], lambda k: xT_lo[:, k, :], 213),
                    "read": read}

        def v_job(g):
            def read(bank, done):
                src = bank[:, :].rearrange("p (j h d) -> p j h d", j=QT, h=GH)
                hi, lo = v[:, g % 2, :, :, 0:HD], v[:, g % 2, :, :, HD:2 * HD]
                free = [T["pv_group", g - 2]] if g >= 2 else []
                act.wait(done, *free)
                a = act.run(lambda e: e.activation(hi, src, ACT.Copy), s_side_act)
                dve.wait(a, *free)
                T["v", g] = d = dve.run(lambda e: e.tensor_tensor(lo, src, hi.bitcast(F32), ALU.subtract), s_side_dve)
                return [a, d]
            return {"name": ("V", g), "need": [("vT", g)],
                    "matmuls": transposes(lambda j: vT[:, j * P:(j + 1) * P]), "read": read}

        def oT_job(t):
            b, i = divmod(t, QT)
            free = (lambda: [T["OP", t - 1]]) if t else (lambda: [])
            return {"name": ("OT", t), "need": [("o", b * GPB + m, i) for m in range(GPB)],
                    "matmuls": transposes(lambda k: o_tok[:, b % 2, i, k * P:(k + 1) * P]),
                    "read": split_read(oT_hi[:, :, :].rearrange("p k n -> p (k n)"),
                                       oT_lo[:, :, :].rearrange("p k n -> p (k n)"), ("OT", t), free, free)}

        def layer_norm(src, dst, slot, sig, free=()):
            def moments():
                dve.wait(T["ln_in", slot])
                a = dve.run(lambda e: e.bn_stats(stats[:, slot % 2, :], src), sig)
                dve.wait(a)
                a = dve.run(lambda e: e.bn_aggr(mv[:, slot % 2, :], stats[:, slot % 2, :]), sig)
                pool.wait(a)
                a = pool.run(lambda e: e.tensor_scalar(rstd[:, slot % 2, 0:1], mv[:, slot % 2, 1:2], EPS, None,
                                                       ALU.add), s_side_pool)
                pool.wait(a, T["mhalf"])
                T["rstd", slot] = pool.run(lambda e: e.tensor_tensor(rstd[:, slot % 2, 1:2], rstd[:, slot % 2, 0:1],
                                                                     mhalf[:, :], ALU.pow), s_side_pool)

            def normalise():
                dve.wait(T["rstd", slot], *free)
                T["ln", slot] = dve.run(lambda e: e.tensor_scalar(
                    dst, src, mv[:, slot % 2, 0:1], rstd[:, slot % 2, 1:2], ALU.subtract, ALU.mult), sig)
            return moments, normalise

        T["mhalf"] = T["zero"]

        def o_project_job(t):
            b, i = divmod(t, QT)

            def read(bank, done):
                dve.wait(done, T["x+bo", b])
                T["ln_in", t] = T["res", t] = a = dve.run(lambda e: e.tensor_tensor(
                    res[:, :], bank[:, :], x_tok[:, b % 2, i, :], ALU.add), s_side_dve)
                return [a]

            moments, normalise = layer_norm(res[:, :], x1[:, t, 0:D], t, s_side_dve,
                                            [T["wlo", n] for n in range(4)])
            return {"name": ("OP", t), "need": [("OT", t, "hi"), ("OT", t, "lo"), ("whi", WO), ("wlo", WO)],
                    "matmuls": hi_lo_products(lambda k: oT_hi[:, k, :], lambda k: oT_lo[:, k, :],
                                              lambda k: w_hi[:, WO, k, :], lambda k: w_lo[:, WO, k, :], 213),
                    "read": read, "later": [moments, normalise]}

        def x1T_job(t):
            def read(bank, done):
                act.wait(done, *([T["logit", t - 1]] if t else []))
                T["x1T", t] = a = act.run(lambda e: e.activation(x1T[:, :, :].rearrange("p k n -> p (k n)"),
                                                                 bank[:, :], ACT.Copy), s_side_act)
                return [a]
            return {"name": ("x1t", t), "need": [("ln", t)],
                    "matmuls": transposes(lambda k: x1[:, t, k * P:(k + 1) * P]), "read": read}

        def logit_job(t):
            def read(bank, done):
                dve.wait(done)
                T["logits", t] = a = dve.run(lambda e: e.tensor_tensor(logits[:, t, :], bank[:, 0:NE], br_row[:, :],
                                                                       ALU.add), s_side_dve)
                return [a]
            return {"name": ("logit", t), "need": [("x1T", t)],
                    "matmuls": [(107, lambda e, bank, k=k: e.matmul(bank[:, 0:NE], x1T[:, k, :], wr[:, k, :],
                                                                    start=(k == 0), stop=(k == KT - 1)))
                                for k in range(KT)], "read": read}

        units = [(g, i, h) for g in range(NG) for i in range(QT) for h in range(GH)]

        def unit_scores(u):
            g, i, h = units[u]
            rows, width = slice(h * HD, (h + 1) * HD), (i + 1) * P
            bank = banks[u % 2]
            pe.wait(ticket("Q", g, "lo"), ticket("K", g, "lo"))
            if u >= 2:
                pe.wait(T["biased", u - 2])
            q, k = slice(i * P, (i + 1) * P), slice(0, width)
            for n, (a, c) in enumerate(((qk_hi, qk_hi), (qk_lo, qk_hi), (qk_hi, qk_lo))):
                T["s", u] = pe.run(lambda e, n=n, a=a, c=c: e.matmul(
                    bank[:, 0:width], a[rows, g % 2, 1, q], c[rows, g % 2, 0, k], start=(n == 0), stop=(n == 2)),
                    s_scores if n == 2 else None)
            if i == QT - 1 and h == GH - 1:
                T["scores", g] = T["s", u]
            dve.wait(T["s", u], T["const2"])
            if u >= 2:
                dve.wait(T["exp", u - 2])
            T["biased", u] = dve.run(lambda e: e.tensor_tensor_reduce(
                out=scores[:, u % 2, 0:width], in0=bank[:, 0:width], in1=dist[:, SEQ - width:SEQ],
                scale=-SLOPE[(g % GPB) * GH + h], scalar=3e38, op0=ALU.add, op1=ALU.min,
                accum_out=neg_max[:, u % 4:u % 4 + 1]), s_biased)
            act.wait(T["biased", u])
            if u >= 2:
                act.wait(T["pT", u - 2])
            q2 = (g * QT + i) % 2
            if h == 0 and g * QT + i >= 2:
                act.wait(T["inv", g * QT + i - 2])
            T["exp", u] = act.run(lambda e: e.activation(
                probs[:, u % 2, 0:width], scores[:, u % 2, 0:width], ACT.Exp, scale=-1.0,
                bias=neg_max[:, u % 4:u % 4 + 1], accum_out=row_sum[:, q2, h:h + 1]), s_exp)

        def unit_transpose(u):
            g, i, h = units[u]
            width = (i + 1) * P
            bank = banks[2 + u % 2]
            pe.wait(T["exp", u])
            if u >= 2:
                pe.wait(T["pThi", u - 2], T["pTlo", u - 2])
            for j in range(i + 1):
                T["pT", u] = pe.run(lambda e, j=j: e.transpose(
                    bank[:, j * P:(j + 1) * P], probs[:, u % 2, j * P:(j + 1) * P], ident[:, :]),
                    s_pT if j == i else None)
            hi, lo = pT_hi[:, u % 2, 0:width], pT_lo[:, u % 2, 0:width]
            free = [T["pv", u - 2]] if u >= 2 else []
            act.wait(T["pT", u], *free)
            T["pThi", u] = act.run(lambda e: e.activation(hi, bank[:, 0:width], ACT.Copy), s_pThi)
            dve.wait(T["pThi", u], *free)
            T["pTlo", u] = dve.run(lambda e: e.tensor_tensor(lo, bank[:, 0:width], hi.bitcast(F32),
                                                             ALU.subtract), s_pTlo)

        def unit_values(u):
            g, i, h = units[u]
            qi = g * QT + i
            bank = banks[4 + qi % 2]
            pe.wait(T["pTlo", u], ticket("v", g))
            if h == 0 and qi >= 2:
                pe.wait(T["pvsum", qi - 2])
            for j in range(i + 1):
                blk = slice(j * P, (j + 1) * P)
                pe.run(lambda e, j=j, blk=blk: e.matmul(
                    bank[:, h * 2 * HD:(h + 1) * 2 * HD], pT_hi[:, u % 2, blk], v[:, g % 2, j, h, :],
                    start=(j == 0), stop=False))
                T["pv", u] = pe.run(lambda e, j=j, blk=blk: e.matmul(
                    bank[:, h * 2 * HD:h * 2 * HD + HD], pT_lo[:, u % 2, blk], v[:, g % 2, j, h, 0:HD],
                    start=False, stop=(j == i)), s_pv if j == i else None)
            if i == QT - 1 and h == GH - 1:
                T["pv_group", g] = T["pv", u]
            if h < GH - 1:
                return
            parts = bank[:, 0:2 * P].rearrange("p (h s d) -> p h s d", h=GH, s=2)
            act.wait(T["pv", u])
            if qi >= 2:
                act.wait(T["pvsum", qi - 2])
            T["pvhi", qi] = act.run(lambda e: e.activation(pv_hi[:, qi % 2, :, :], parts[:, :, 0, :], ACT.Copy), s_pvhi)
            dve.wait(T["exp", u])
            if qi >= 2:
                dve.wait(T["o", (qi - 2) // QT, (qi - 2) % QT])
            T["inv", qi] = dve.run(lambda e: e.reciprocal(row_inv[:, qi % 2, :], row_sum[:, qi % 2, :]), s_inv)
            dve.wait(T["pvhi", qi])
            T["pvsum", qi] = dve.run(lambda e: e.tensor_tensor(pv_sum[:, qi % 2, :, :], parts[:, :, 1, :],
                                                               pv_hi[:, qi % 2, :, :], ALU.add), s_pvsum)
            b, m = divmod(g, GPB)
            pool.wait(T["pvsum", qi], T["inv", qi])
            if b >= 2:
                pool.wait(ticket("OT", (b - 2) * QT + i))
            T["o", g, i] = pool.run(lambda e: e.tensor_tensor(
                o_tok[:, b % 2, i, m * P:(m + 1) * P].rearrange("p (h d) -> p h d", h=GH), pv_sum[:, qi % 2, :, :],
                row_inv[:, qi % 2, :].unsqueeze(2).to_broadcast([P, GH, HD]), ALU.mult), s_o)

        split_weight(WK, act, dve, T["w", WK])
        for k in range(KT):
            queue.append(xT_job(0, k))
        side_work(1e9)
        flush()
        queue.append(project_job("K", 0))
        T["wq_ready"] = T["wq"]
        side_work(1e9)
        split_weight(WQ, act, dve, T["wq"])
        split_weight(WV, act, dve, T["w", WV])
        flush()
        for job in (project_job("Q", 0), project_job("VT", 0)):
            queue.append(job)
        side_work(1e9)
        queue.append(v_job(0))
        side_work(1e9)
        split_weight(WO, pool, pool, T["w", WO])

        def add_bias_to_x(b):
            pool.wait(*[T["xT", b, k] for k in range(KT)])
            for j in range(QT):
                T["x+bo", b] = pool.run(lambda e, j=j: e.tensor_tensor(
                    x_tok[:, b % 2, j, :], x_tok[:, b % 2, j, :], bo_row[:, :], ALU.add), s_side_pool)
            if b + 1 < NB and b >= 1:
                pass

        add_bias_to_x(0)

        lazy = deque()
        for u in range(len(units) + 2):
            if u < len(units):
                g, i, h = units[u]
                step = i * GH + h
                if step == 0:
                    side_work(1e9 if queue else 0)
                    if g + 1 < NG:
                        for kind in ("K", "Q", "VT"):
                            queue.append(project_job(kind, g + 1))
                        queue.append(v_job(g + 1))
                        if (g + 2) % GPB == 0 and g + 2 < NG:
                            b = (g + 2) // GPB
                            for k in range(KT):
                                queue.append(xT_job(b, k))
                    if g % GPB == 0 and g:
                        b = g // GPB - 1
                        lazy.extend(range(b * QT, (b + 1) * QT))
                if lazy and step % 8 == 4:
                    t = lazy.popleft()
                    queue.extend((oT_job(t), o_project_job(t), x1T_job(t), logit_job(t)))
                unit_scores(u)
            if 1 <= u <= len(units):
                unit_transpose(u - 1)
            flush()
            flush_later(2)
            if u < len(units):
                side_work(queued_cost() / (GH * QT - step))
            if u >= 2:
                unit_values(u - 2)
            if u < len(units) and step == GH * QT - 1:
                if g % GPB == 2 and g // GPB + 1 < NB:
                    b = g // GPB + 1
                    side_work(1e9)
                    flush()
                    add_bias_to_x(b)
                if g % GPB == 1 and g // GPB >= 1 and g // GPB + 1 < NB:
                    b = g // GPB + 1
                    if b >= 2:
                        sp.wait(ticket("res", (b - 2) * QT + QT - 1))
                        T["x", b] = load_x(b)
        lazy.extend(range(NT - QT, NT))
        while lazy:
            t = lazy.popleft()
            queue.extend((oT_job(t), o_project_job(t), x1T_job(t), logit_job(t)))
        side_work(1e9)
        flush()
        flush_later()

        def rt(n):
            return route[:, n, :, :]

        def r_op(make, *waits):
            dve.wait(*waits)
            t = dve.run(make, s_route)
            dve.wait(t)
            return t

        EQ, DIFF, EXPD, HOT, FREE_, RANK, TOT, SCAN_A, SCAN_B, POS, TILES, TMP = range(12)
        mx = route[:, FREE_, :, 0]
        T["mx"] = r_op(lambda e: e.tensor_reduce(mx, logits[:, :, :], AX_X, ALU.max), T["logits", NT - 1])
        r_op(lambda e: e.tensor_tensor(rt(EQ), logits[:, :, :], mx.unsqueeze(2).to_broadcast([P, NT, NE]), ALU.is_equal))
        T["diff"] = r_op(lambda e: e.tensor_tensor(rt(DIFF), logits[:, :, :],
                                                   mx.unsqueeze(2).to_broadcast([P, NT, NE]), ALU.subtract))
        act.wait(T["diff"])
        T["expd"] = act.run(lambda e: e.activation(rt(EXPD), rt(DIFF), ACT.Exp), s_side_act)
        taken = route[:, TMP, :, 0]
        r_op(lambda e: e.tensor_copy(route[:, HOT, :, 0], route[:, EQ, :, 0]))
        r_op(lambda e: e.tensor_scalar(taken, route[:, EQ, :, 0], -1.0, 1.0, ALU.mult, ALU.add))
        for j in range(1, NE):
            T["hot"] = r_op(lambda e, j=j: e.tensor_tensor(route[:, HOT, :, j], route[:, EQ, :, j], taken, ALU.mult))
            if j < NE - 1:
                r_op(lambda e, j=j: e.tensor_tensor(taken, taken, route[:, HOT, :, j], ALU.subtract))
        hot = rt(HOT).rearrange("p t e -> p (t e)")
        pe.wait(T["hot"])
        pe.run(lambda e: e.matmul(banks[0][:, 0:NT * NE], before[:, :], hot, start=True, stop=True))
        T["rank"] = pe.run(lambda e: e.matmul(banks[1][:, 0:NT * NE], ones[:, :], hot, start=True, stop=True), s_side)
        bank_te = [banks[n][:, 0:NT * NE].rearrange("p (t e) -> p t e", e=NE) for n in range(2)]
        r_op(lambda e: e.tensor_copy(rt(TOT), bank_te[1]), T["rank"])
        r_op(lambda e: e.tensor_copy(rt(SCAN_A), bank_te[1]))
        src, dst, step = SCAN_A, SCAN_B, 1
        while step < NT:
            r_op(lambda e, s=src, d=dst, n=step: e.tensor_copy(route[:, d, 0:n, :], route[:, s, 0:n, :]))
            r_op(lambda e, s=src, d=dst, n=step: e.tensor_tensor(route[:, d, n:NT, :], route[:, s, n:NT, :],
                                                                 route[:, s, 0:NT - n, :], ALU.add))
            src, dst, step = dst, src, 2 * step
        full = route[:, EQ, :, :].rearrange("p t e -> p (t e)").rearrange("p (e t) -> p e t", e=NE)
        count = route[:, src, NT - 1, :]
        r_op(lambda e: e.tensor_tensor(full, count.unsqueeze(2).to_broadcast([P, NE, NT]),
                                       small[:, C_FULL:C_FULL + NT].unsqueeze(1).to_broadcast([P, NE, NT]), ALU.is_gt))
        ends = route[:, TILES, 0, :]
        r_op(lambda e: e.tensor_reduce(ends, full, AX_X, ALU.add))
        for j in range(1, NE):
            r_op(lambda e, j=j: e.tensor_tensor(ends[:, j:j + 1], ends[:, j:j + 1], ends[:, j - 1:j], ALU.add))
        begins = route[:, TILES, 1, :]
        r_op(lambda e: e.memset(begins[:, 0:1], 0.0))
        r_op(lambda e: e.tensor_scalar(begins[:, 1:NE], ends[:, 0:NE - 1], float(P), None, ALU.mult))
        past = route[:, DIFF, :, :].rearrange("p t e -> p (t e)")[:, 0:NS * (NE - 1)].rearrange("p (s e) -> p s e", e=NE - 1)
        r_op(lambda e: e.tensor_tensor(past, small[:, C_SLOT:C_SLOT + NS].unsqueeze(2).to_broadcast([P, NS, NE - 1]),
                                       ends[:, 0:NE - 1].unsqueeze(1).to_broadcast([P, NS, NE - 1]), ALU.is_ge),
             T["expd"])
        past_sum = route[:, EQ, :, :].rearrange("p t e -> p (t e)")[:, 0:NS]
        r_op(lambda e: e.tensor_reduce(past_sum, past, AX_X, ALU.add))
        T["slot_expert"] = r_op(lambda e: e.tensor_scalar(slot_expert[:, :], past_sum, float(2 * P), None, ALU.mult))
        r_op(lambda e: e.tensor_tensor(rt(POS), rt(src), rt(TOT), ALU.subtract))
        r_op(lambda e: e.tensor_tensor(rt(POS), rt(POS), bank_te[0], ALU.add))
        r_op(lambda e: e.tensor_tensor(rt(POS), rt(POS), begins.unsqueeze(1).to_broadcast([P, NT, NE]), ALU.add))
        r_op(lambda e: e.tensor_tensor(rt(POS), rt(POS), rt(HOT), ALU.mult))
        r_op(lambda e: e.tensor_reduce(route[:, TMP, :, 0], rt(POS), AX_X, ALU.add))
        T["position"] = r_op(lambda e: e.tensor_copy(position[:, :], route[:, TMP, :, 0]))
        r_op(lambda e: e.tensor_reduce(route[:, TMP, :, 1], rt(EXPD), AX_X, ALU.add))
        r_op(lambda e: e.reciprocal(x1[:, :, D], route[:, TMP, :, 1]))
        T["rows_ready"] = r_op(lambda e: e.tensor_copy(x1[:, :, D + 1], small[:, C_TOKEN:C_TOKEN + NT]))
        r_op(lambda e: e.memset(x1[:, :, D + 2:D + 4], 0.0))

        s_scatter = signal("rows_scattered")
        pool.wait(T["position"], (s_route, s_route.value), T["scratch"])
        for t in range(NT):
            T["scattered"] = pool.run(lambda e, t=t: e.indirect_dma_start(
                out=xs_dram, out_offset=bass.IndirectOffsetOnAxis(ap=position[:, t:t + 1].bitcast(U32), axis=0),
                in_=x1[:, t, :], in_offset=None, bounds_check=NS * P - 1, oob_is_err=False), s_scatter, 16)

        p2 = Map(nc, x1_map.at)
        y = p2.put("y", [P, NS, D], F32)
        xsT_hi = p2.put("xsT_hi", [P, NS, KT, P], F32R)
        xsT_lo = p2.put("xsT_lo", [P, NS, KT, P], F32R)
        up_w = [[p2.put(f"up_{part}{k}", [P, NE, 2 * P], F32R) for k in range(KT)] for part in ("hi", "lo")]
        down_w = [p2.put(f"down_{part}", [P, NE, D], F32R) for part in ("hi", "lo")]
        NUPS = 2
        up_raw = p2.put("up_raw", [P, NUPS, KT, 2, P], F32)
        assert p2.at <= nc._sbuf_addr_for_side("right"), p2.at
        p3 = Map(nc, keep.at)
        hT_hi = p3.put("hT_hi", [P, NS, P], F32R)
        hT_lo = p3.put("hT_lo", [P, NS, P], F32R)
        silu = p3.put("silu", [P, 2, 2, P], F32)
        h_tok = p3.put("h_tok", [P, 2, 2, P], F32)
        NDS = 4
        down_raw = p3.put("down_raw", [P, NDS, D], F32)
        assert p3.at <= x1_map.at
        LN_BUFS = 4
        fin = Map(nc, up_raw_at := p2.at - 4 * NUPS * KT * 2 * P)
        out_rows_sb = [fin.put(f"out_row{n}", [P, D], F32) for n in range(LN_BUFS)]
        fin2 = Map(nc, p3.at - 4 * NDS * D)
        xs_back = [fin2.put(f"xs_back{n}", [P, D], F32) for n in range(NDS)]

        s_upraw = [signal(f"up_raw_loaded{n}") for n in range(NUPS)]
        s_downraw = [signal(f"down_raw_loaded{n}") for n in range(NDS)]
        s_rows = [signal(f"rows_loaded{n}") for n in range(5)]
        s_meta = signal("meta_loaded")
        s_token = signal("token_numbers")
        s_upw_hi, s_upw_lo = signal("up_hi"), signal("up_lo")
        s_dw_hi, s_dw_lo = signal("down_hi"), signal("down_lo")
        s_xsT, s_xsT_hi, s_xsT_lo = signal("xsT"), signal("xsT_hi_done"), signal("xsT_lo_done")
        s_up, s_silu, s_h, s_hT, s_hThi, s_hTlo = (signal(n) for n in (
            "up_products", "silu_done", "h_done", "hT_done", "hT_hi_done", "hT_lo_done"))
        s_down, s_y = signal("down_products"), signal("y_added")
        s_fin, s_rstd, s_back = signal("final_dve"), signal("final_pool"), [signal(f"xs_back{n}") for n in range(NDS)]
        s_out = [signal(f"out_written{n}") for n in range(LN_BUFS)]

        phase1_done = [T["mx"]]
        route_done = (s_route, s_route.value)

        def load_up(c, e):
            n = (c * NE + e) % NUPS
            sp.wait(*phase1_done, route_done)
            if c * NE + e >= NUPS:
                prev = c * NE + e - NUPS
                sp.wait(T["uphi", prev], T["uplo", prev])
            cols = slice(c * P, (c + 1) * P)
            for half, W in enumerate((Wg, Wu)):
                T["upraw", c * NE + e] = load(up_raw[:, n, :, half, :],
                                              W[e].rearrange("(k p) f -> p k f", p=P)[:, :, cols], s_upraw[n])

        def split_up(c, e):
            n = (c * NE + e) % NUPS
            idx = c * NE + e
            free = [T["up_chunk", c - 1]] if c else []
            for k in range(KT):
                src = up_raw[:, n, k, :, :].rearrange("p g f -> p (g f)")
                act.wait(T["upraw", idx], *free)
                T["uphi", idx] = act.run(lambda e_, k=k, src=src: e_.activation(up_w[0][k][:, e, :], src, ACT.Copy),
                                         s_upw_hi)
                lane, sig = dve, s_upw_lo
                lane.wait(T["uphi", idx], T["upraw", idx], *free)
                T["uplo", idx] = lane.run(lambda e_, k=k, src=src: e_.tensor_tensor(
                    up_w[1][k][:, e, :], src, up_w[0][k][:, e, :].bitcast(F32), ALU.subtract), sig)

        def load_down(c, e):
            idx = c * NE + e
            n = idx % NDS
            sp.wait(*phase1_done, T["scattered"])
            if idx >= NDS:
                sp.wait(T["dhi", idx - NDS], T["dlo", idx - NDS])
            T["draw", idx] = load(down_raw[:, n, :], Wd[e, c * P:(c + 1) * P, :], s_downraw[n])

        def split_down(c, e):
            idx = c * NE + e
            src = down_raw[:, idx % NDS, :]
            free = [T["down_chunk", c - 1]] if c else []
            act.wait(T["draw", idx], *free)
            T["dhi", idx] = act.run(lambda e_: e_.activation(down_w[0][:, e, :], src, ACT.Copy), s_dw_hi)
            dve.wait(T["dhi", idx], T["draw", idx], *free)
            T["dlo", idx] = dve.run(lambda e_: e_.tensor_tensor(down_w[1][:, e, :], src,
                                                                down_w[0][:, e, :].bitcast(F32), ALU.subtract), s_dw_lo)

        act.wait(*phase1_done, route_done)
        pool.wait(*phase1_done)
        pe.wait(*phase1_done)
        for e in range(NUPS):
            load_up(0, e)
        sp.wait(T["scattered"], route_done)
        for n, s0 in enumerate(range(0, NS, 4)):
            s1 = min(s0 + 4, NS)
            T["rows", n] = load(y[:, s0:s1, :], xs_rows[:, s0:s1, 0:D], s_rows[n])
        T["meta"] = load(meta[:, :, :], xs_rows[:, :, D:ROW], s_meta)
        for e in range(NE):
            split_up(0, e)
            if e + NUPS < NE:
                load_up(0, e + NUPS)
        for e in range(NE):
            load_down(0, e)

        def split_rows(s):
            bank = banks[4 + s % 2]
            pe.wait(T["rows", s // 4])
            if s >= 2:
                pe.wait(T["xsTlo", s - 2])
            for k in range(KT):
                T["xsT", s] = pe.run(lambda e, k=k: e.transpose(bank[:, k * P:(k + 1) * P], y[:, s, k * P:(k + 1) * P],
                                                                ident[:, :]), s_xsT if k == KT - 1 else None)
            hi = xsT_hi[:, s, :, :].rearrange("p k n -> p (k n)")
            lo = xsT_lo[:, s, :, :].rearrange("p k n -> p (k n)")
            act.wait(T["xsT", s])
            T["xsThi", s] = act.run(lambda e: e.activation(hi, bank[:, :], ACT.Copy), s_xsT_hi)
            dve.wait(T["xsThi", s])
            T["xsTlo", s] = dve.run(lambda e: e.tensor_tensor(lo, bank[:, :], hi.bitcast(F32), ALU.subtract), s_xsT_lo)

        pairs = [tuple(s for s in (s0, s0 + 1) if s < NS) for s0 in range(0, NS, 2)]
        U_BANKS, T_BANKS, D_BANKS = (0, 1, 7), (2, 3), (4, 5, 6)
        count_u = {"pair": 0, "down": 0}
        registers, at = {}, {}

        def load_offset(eng, s):
            registers[s] = eng.alloc_register(f"slot{s}_expert")
            eng.load(registers[s], slot_expert[0:1, s:s + 1])

        def take_offset(eng, s, times):
            at[0] = eng.snap(registers[s], min_val=0, max_val=(NE - 1) * 2 * P) * times

        def up_pair(c, pr):
            idx = c * len(pairs) + pr
            slots = pairs[pr]
            bank = banks[U_BANKS[idx % 3]]
            if idx >= 3:
                pe.wait(T["h", idx - 3])
            for n, s in enumerate(slots):
                if c == 0:
                    split_rows(s)
                    pe.wait(T["xsTlo", s])
                    pe.run(lambda e, s=s: load_offset(e, s))
                pe.run(lambda e, s=s: take_offset(e, s, 1))
                seq = [(a, w, k) for k in range(KT) for a, w in ((xsT_hi, 0), (xsT_lo, 0), (xsT_hi, 1))]
                for q, (a, w, k) in enumerate(seq):
                    last = q == len(seq) - 1
                    T["up", idx] = pe.run(lambda e, s=s, n=n, q=q, a=a, w=w, k=k, last=last: e.matmul(
                        bank[:, n * 2 * P:(n + 1) * 2 * P], a[:, s, k, :],
                        up_w[w][k][:, :, :].rearrange("p a f -> p (a f)")[:, bass.ds(at[0], 2 * P)],
                        start=(q == 0), stop=last), s_up if last and n == len(slots) - 1 else None)
            m = len(slots)
            gu = bank[:, 0:m * 2 * P].rearrange("p (s g f) -> p s g f", s=m, g=2)
            act.wait(T["up", idx])
            if idx >= 2:
                act.wait(T["h", idx - 2])
            T["silu", idx] = act.run(lambda e: e.activation(silu[:, idx % 2, 0:m, :], gu[:, :, 0, :], ACT.Silu), s_silu)
            dve.wait(T["silu", idx])
            if idx >= 2:
                dve.wait(T["hT", idx - 2])
            T["h", idx] = dve.run(lambda e: e.tensor_tensor(h_tok[:, idx % 2, 0:m, :], gu[:, :, 1, :],
                                                            silu[:, idx % 2, 0:m, :], ALU.mult), s_h)

        def transpose_pair(c, pr):
            idx = c * len(pairs) + pr
            slots = pairs[pr]
            m = len(slots)
            bank = banks[T_BANKS[idx % 2]]
            pe.wait(T["h", idx])
            if idx >= 2:
                pe.wait(T["hTlo", idx - 2])
            for n in range(m):
                T["hT", idx] = pe.run(lambda e, n=n: e.transpose(bank[:, n * P:(n + 1) * P], h_tok[:, idx % 2, n, :],
                                                                 ident[:, :]), s_hT if n == m - 1 else None)
            hi = hT_hi[:, slots[0]:slots[0] + m, :].rearrange("p s f -> p (s f)")
            lo = hT_lo[:, slots[0]:slots[0] + m, :].rearrange("p s f -> p (s f)")
            free = [T["down_chunk", c - 1]] if c else []
            act.wait(T["hT", idx], *free)
            T["hThi", idx] = act.run(lambda e: e.activation(hi, bank[:, 0:m * P], ACT.Copy), s_hThi)
            dve.wait(T["hThi", idx], *free)
            T["hTlo", idx] = dve.run(lambda e: e.tensor_tensor(lo, bank[:, 0:m * P], hi.bitcast(F32), ALU.subtract), s_hTlo)

        def down_slot(c, s):
            idx = c * NS + s
            bank = banks[D_BANKS[idx % 3]]
            pe.wait(T["hTlo", c * len(pairs) + s // 2])
            if idx >= 3:
                pe.wait(T["y", idx - 3])
            pe.run(lambda e: take_offset(e, s, D // (2 * P)))
            for q, (a, w) in enumerate(((hT_hi, 0), (hT_lo, 0), (hT_hi, 1))):
                T["down", idx] = pe.run(lambda e, q=q, a=a, w=w: e.matmul(
                    bank[:, :], a[:, s, :], down_w[w][:, :, :].rearrange("p a f -> p (a f)")[:, bass.ds(at[0], D)],
                    start=(q == 0), stop=(q == 2)), s_down if q == 2 else None)
            dve.wait(T["down", idx])
            if c == 0:
                T["y", idx] = dve.run(lambda e: e.tensor_copy(y[:, s, :], bank[:, :]), s_y)
            else:
                dve.wait(T["y", idx - NS])
                T["y", idx] = dve.run(lambda e: e.tensor_tensor(y[:, s, :], bank[:, :], y[:, s, :], ALU.add), s_y)

        def final_moments(s):
            nb = s % NDS
            sp.wait(*[T["dlo", NC * NE - 1]])
            if s >= NDS:
                sp.wait(T["res2", s - NDS])
            T["back", s] = load(xs_back[nb][:, :], xs_rows[:, s, 0:D], s_back[nb])
            dve.wait(T["back", s], T["y", (NC - 1) * NS + s], T["meta"])
            T["res2", s] = dve.run(lambda e: e.scalar_tensor_tensor(
                y[:, s, :], y[:, s, :], meta[:, s, 0:1], xs_back[nb][:, :], ALU.mult, ALU.add), s_fin)
            T["ln_in", ("f", s)] = T["res2", s]
            dve.wait(T["res2", s])
            if s >= 2:
                dve.wait(T["fln", s - 2])
            a = dve.run(lambda e: e.bn_stats(stats[:, s % 2, :], y[:, s, :]), s_fin)
            dve.wait(a)
            a = dve.run(lambda e: e.bn_aggr(mv[:, s % 2, :], stats[:, s % 2, :]), s_fin)
            pool.wait(a)
            a = pool.run(lambda e: e.tensor_scalar(rstd[:, s % 2, 0:1], mv[:, s % 2, 1:2], EPS, None, ALU.add), s_rstd)
            pool.wait(a)
            T["frstd", s] = pool.run(lambda e: e.tensor_tensor(rstd[:, s % 2, 1:2], rstd[:, s % 2, 0:1],
                                                               mhalf[:, :], ALU.pow), s_rstd)

        def final_store(s):
            n = s % LN_BUFS
            dve.wait(T["frstd", s], T["uplo", NC * NE - 1])
            if s >= LN_BUFS:
                dve.wait(T["stored", s - LN_BUFS])
            T["fln", s] = dve.run(lambda e: e.tensor_scalar(
                out_rows_sb[n][:, :], y[:, s, :], mv[:, s % 2, 0:1], rstd[:, s % 2, 1:2], ALU.subtract, ALU.mult), s_fin)
            pool.wait(T["fln", s], T["token"])
            T["stored", s] = pool.run(lambda e: e.indirect_dma_start(
                out=out_rows, out_offset=bass.IndirectOffsetOnAxis(ap=token[:, s:s + 1].bitcast(U32), axis=0),
                in_=out_rows_sb[n][:, :], in_offset=None, bounds_check=NT * P - 1, oob_is_err=False), s_out[n], 16)

        for c in range(NC):
            for pr in range(len(pairs) + 1):
                if pr < len(pairs):
                    up_pair(c, pr)
                if pr >= 1:
                    transpose_pair(c, pr - 1)
                if c == 0 and pr == 0:
                    dve.wait(T["meta"])
                    T["token"] = dve.run(lambda e: e.tensor_copy(token[:, :], meta[:, :, 1]), s_token)
                if pr < NE:
                    split_down(c, pr)
                    if c + 1 < NC:
                        load_down(c + 1, pr)
                if c + 1 < NC and pr == 4:
                    for e in range(NUPS):
                        load_up(c + 1, e)
            T["up_chunk", c] = T["up", c * len(pairs) + len(pairs) - 1]
            for s in range(NS):
                down_slot(c, s)
                if c + 1 < NC and s % 4 == 0 and s // 4 < NE:
                    e = s // 4
                    split_up(c + 1, e)
                    if e + NUPS < NE:
                        load_up(c + 1, e + NUPS)
                if c == NC - 1:
                    final_moments(s)
                    if s >= 1:
                        final_store(s - 1)
            T["down_chunk", c] = T["down", c * NS + NS - 1]
        final_store(NS - 1)
        pool.wait(*[T["stored", s] for s in range(NS - LN_BUFS, NS)])

        block = ctx.enter_context(nc.Block())
        block.sync(sp.emit)
        block.gpsimd(pool.emit)
        block.scalar(act.emit)
        block.tensor(pe.emit)
        block.vector(dve.emit)


_INS = ["x", "Wq", "bq", "Wk", "bk", "Wv", "bv", "Wo", "bo"]
_FFN = ["Wr", "br", "Wg", "Wu", "Wd"]


def constants():
    p, c = np.arange(P)[:, None], np.arange(SEQ)[None, :]
    dist = np.where(c - (SEQ - P) > p, MASKED, c - (SEQ - 1)).astype(np.float32)
    scale = np.array([1.0 / (math.sqrt(HD) * s) for s in slopes()], np.float32)
    per_col = np.repeat(scale, HD)
    small = np.zeros((P, N_SMALL), np.float32)
    small[:, C_FULL:C_FULL + NT] = np.arange(NT) * P
    small[:, C_SLOT:C_SLOT + NS] = np.arange(NS)
    small[:, C_TOKEN:C_TOKEN + NT] = np.arange(NT)[None, :] * P + p
    small[:, C_QSCALE:C_QSCALE + KT] = per_col.reshape(KT, P).T
    return {
        "c_ident": np.eye(P, dtype=np.float32),
        "c_dist": dist,
        "c_before": (p < np.arange(P)[None, :]).astype(np.float32),
        "c_small": small,
        "c_qscale": np.broadcast_to(per_col, (P, D)).copy(),
    }


def kernel(**inputs):
    import concourse.bacc as _bacc
    from concourse.bass_utils import run_bass_kernel_spmd as _run

    nc = _bacc.Bacc("TRN2", target_bir_lowering=False, num_devices=1)
    arrays, args = {}, []
    named = [(n, inputs[f"L0_attn_{n}"]) for n in _INS] + [(n, inputs[f"L0_ffn_{n}"]) for n in _FFN]
    for name, a in named + list(constants().items()):
        a = np.ascontiguousarray(a)
        arrays[f"in_{name}_dram"] = a
        args.append(nc.dram_tensor(f"in_{name}_dram", a.shape, mybir.dt.from_np(a.dtype), kind="ExternalInput").ap())
    out = nc.dram_tensor("out_dram", (NB, SEQ, D), F32, kind="ExternalOutput").ap()
    build(nc, *args, out)
    r = _run(nc, [arrays], core_ids=[0])
    return r.results[0]["out_dram"]
```

```python
import math
from collections import deque
from contextlib import ExitStack

import numpy as np

import concourse.bass as bass
from concourse import mybir

F32 = mybir.dt.float32
F32R = mybir.dt.float32r
I32 = mybir.dt.int32
U32 = mybir.dt.uint32
ALU = mybir.AluOpType
ACT = mybir.ActivationFunctionType
AX_X = mybir.AxisListType.X

P = 128
NB, SEQ, D = 4, 512, 512
NH = 16
HD = D // NH
GH = P // HD
KT = D // P
QT = SEQ // P
NG = NB * (NH // GH)
GPB = NH // GH
NT = NB * QT
NE, FF = 4, 2048
NS = NT + NE - 1
NC = FF // P
ROW = D + 4
TRASH = 4095
EPS = 1e-5
MASKED = -1e30
NRS = 4

C_FULL, C_SLOT, C_TOKEN, C_QSCALE = 0, NT, NT + NS, NT + NS + NT
N_SMALL = C_QSCALE + KT


class Signal:

    def __init__(self, ctx, nc, name):
        self.sem = ctx.enter_context(nc.semaphore(name))
        self.value = 0


class Lane:

    def __init__(self):
        self.steps = []
        self.waited = {}

    def wait(self, *tickets):
        for signal, value in tickets:
            if self.waited.get(signal, 0) < value:
                self.waited[signal] = value
                self.steps.append(lambda eng, s=signal.sem, v=value: eng.wait_ge(s, v))

    def run(self, make, signal=None, by=1):
        if signal is None:
            self.steps.append(make)
            return None
        self.steps.append(lambda eng: make(eng).then_inc(signal.sem, by))
        signal.value += by
        return (signal, signal.value)

    def emit(self, eng):
        for step in self.steps:
            step(eng)


class Map:

    def __init__(self, nc, at):
        self.nc, self.at = nc, (at + 31) // 32 * 32

    def put(self, name, shape, dtype):
        t = self.nc.alloc_sbuf_tensor_at(name, shape, dtype, offset=self.at)
        self.at += (4 * int(np.prod(shape[1:])) + 31) // 32 * 32
        return t


def slopes():
    start = 2 ** (-2 ** (-(math.log2(NH) - 3)))
    return [float(np.float32(start * start ** i)) for i in range(NH)]


def build(nc, x, Wq, bq, Wk, bk, Wv, bv, Wo, bo, Wr, br, Wg, Wu, Wd,
          c_ident, c_dist, c_before, c_small, c_qscale, out):
    SLOPE = slopes()
    xs_dram = nc.dram_tensor("xs_scratch", (NS * P, ROW), F32, kind="Internal").ap()
    x_rows = x.rearrange("b (t p) d -> b p t d", p=P)
    out_rows = out.rearrange("b t d -> (b t) d")
    xs_rows = xs_dram.rearrange("(s p) d -> p s d", p=P)

    with ExitStack() as ctx:
        ctx.enter_context(nc.allow_non_contiguous_dma(reason="small vectors laid across partitions"))

        def signal(name):
            return Signal(ctx, nc, name)

        banks = [ctx.enter_context(nc.psum_tensor(f"bank{i}", [P, 512], F32)) for i in range(8)]
        pe, act, dve, pool, sp = (Lane() for _ in range(5))

        base = nc._sbuf_addr_for_side("left")
        keep = Map(nc, base)
        ident = keep.put("ident", [P, P], F32)
        small = keep.put("small", [P, N_SMALL], F32)
        logits = keep.put("logits", [P, NT, NE], F32)
        slot_expert = keep.put("slot_expert", [P, NS], I32)
        position = keep.put("position", [P, NT], I32)
        meta = keep.put("meta", [P, NS, 4], F32)
        token = keep.put("token", [P, NS], I32)
        stats = keep.put("stats", [P, 2, 6], F32)
        mv = keep.put("mv", [P, 2, 2], F32)
        rstd = keep.put("rstd", [P, 2, 2], F32)
        mhalf = keep.put("mhalf", [P, 1], F32)

        x1_map = Map(nc, keep.at)
        x1 = x1_map.put("x1", [P, NT, ROW], F32)
        w_raw = Map(nc, keep.at).put("w_raw", [P, 4, KT, D], F32)

        p1 = Map(nc, x1_map.at)
        WK, WQ, WV, WO = range(4)
        w_hi = p1.put("w_hi", [P, 4, KT, D], F32R)
        w_lo = p1.put("w_lo", [P, 4, KT, D], F32R)
        dist = p1.put("dist", [P, SEQ], F32)
        x_tok = p1.put("x_tok", [P, 2, QT, D], F32)
        xT_hi = p1.put("xT_hi", [P, KT, SEQ], F32R)
        xT_lo = p1.put("xT_lo", [P, KT, SEQ], F32R)
        qk_hi = p1.put("qk_hi", [P, 2, 2, SEQ], F32R)
        qk_lo = p1.put("qk_lo", [P, 2, 2, SEQ], F32R)
        vT = p1.put("vT", [P, SEQ], F32)
        v = p1.put("v", [P, 2, QT, GH, 2 * HD], F32R)
        route = Map(nc, p1.at).put("route", [P, 12, NT, NE], F32)
        scores = p1.put("scores", [P, 2, SEQ], F32)
        probs = p1.put("probs", [P, 2, SEQ], F32)
        pT_hi = p1.put("pT_hi", [P, 2, SEQ], F32R)
        pT_lo = p1.put("pT_lo", [P, 2, SEQ], F32R)
        filler_row = Map(nc, p1.at).put("filler_row", [P, ROW], F32)
        o_tok = p1.put("o_tok", [P, 2, QT, D], F32)
        oT_hi = p1.put("oT_hi", [P, KT, P], F32R)
        oT_lo = p1.put("oT_lo", [P, KT, P], F32R)
        res = p1.put("res", [P, D], F32)
        x1T = p1.put("x1T", [P, KT, P], F32)
        pvT = p1.put("pvT", [2 * HD, SEQ], F32)
        bo_row = p1.put("bo_row", [P, D], F32)
        pv_hi = p1.put("pv_hi", [P, 2, QT, HD], F32)
        pv_sum = p1.put("pv_sum", [P, 2, QT, HD], F32)
        bias_col = p1.put("bias_col", [P, 3, GPB], F32)
        wr = p1.put("wr", [P, KT, NE], F32)
        br_row = p1.put("br_row", [P, NE], F32)
        neg_max = p1.put("neg_max", [P, 2, QT], F32)
        row_sum = p1.put("row_sum", [P, NRS, QT], F32)
        row_inv = p1.put("row_inv", [P, 2, QT], F32)
        qscale = p1.put("qscale", [P, D], F32)
        before = p1.put("before", [P, P], F32)
        ones = p1.put("ones", [P, P], F32)
        assert p1.at <= nc._sbuf_addr_for_side("right"), p1.at

        s_x = [signal(f"x_loaded{i}") for i in range(2)]
        s_w = [signal(f"w_loaded{i}") for i in range(4)]
        s_const, s_const2 = signal("constants_loaded"), signal("late_constants_loaded")
        s_fill = signal("scratch_prefilled")
        s_pool = signal("pool_setup")
        s_whi, s_wlo = signal("w_hi_done"), signal("w_lo_done")
        s_scores, s_biased, s_exp = signal("scores_done"), signal("biased_done"), signal("exp_done")
        s_pT, s_pThi, s_pTlo = signal("pT_done"), signal("pT_hi_done"), signal("pT_lo_done")
        s_pv, s_pvhi, s_pvsum, s_o = signal("pv_done"), signal("pv_hi_copied"), signal("pv_summed"), signal("o_done")
        s_pvT, s_back_tr = signal("pvT_copied"), signal("values_transposed")
        s_inv = signal("row_inverse_done")
        s_side = signal("side_products_done")
        s_side_act, s_side_dve, s_side_pool = signal("side_act"), signal("side_dve"), signal("side_pool")
        s_route = signal("route_dve")

        T = {}

        def load(dst, src, sig, lane=sp):
            return lane.run(lambda e: e.dma_start(dst, src), sig, 16)

        def load_x(b):
            return load(x_tok[:, b % 2, :, :], x_rows[b], s_x[b % 2])

        T["x", 0] = load_x(0)
        for t, src in ((ident[:, :], c_ident), (small[:, :], c_small)):
            load(t, src, s_const)
        for n, vec in enumerate((bk, bq, bv)):
            load(bias_col[:, n, :], vec.rearrange("(m p) -> p m", p=P), s_const)
        T["const"] = load(qscale[:, :], c_qscale, s_const)
        for n, W in ((WK, Wk), (WQ, Wq), (WV, Wv), (WO, Wo)):
            T["w", n] = load(w_raw[:, n, :, :], W.rearrange("(k p) n -> p k n", p=P), s_w[n])
            if n == WK:
                load(dist[:, :], c_dist, s_const2)
                load(before[:, :], c_before, s_const2)
                load(bo_row[:, :], bo.partition_broadcast(P), s_const2)
                load(br_row[:, :], br.partition_broadcast(P), s_const2)
                T["const2"] = load(wr[:, :, :], Wr.rearrange("(k p) e -> p k e", p=P), s_const2)
        T["x", 1] = load_x(1)

        pool.run(lambda e: e.memset(mhalf[:, :], -0.5), s_pool)
        pool.run(lambda e: e.memset(ones[:, :], 1.0), s_pool)
        T["zero"] = pool.run(lambda e: e.memset(filler_row[:, :], 0.0), s_pool)
        pool.wait(T["zero"])
        T["fill"] = pool.run(lambda e: e.memset(filler_row[:, D + 1:D + 2], float(TRASH)), s_pool)
        pool.wait(T["const2"])
        T["bq"] = pool.run(lambda e: e.tensor_tensor(bias_col[:, 1, :], bias_col[:, 1, :],
                                                     small[:, C_QSCALE:C_QSCALE + KT], ALU.mult), s_pool)
        pool.wait(T["w", WQ])
        for k in range(KT):
            T["wq"] = pool.run(lambda e, k=k: e.tensor_tensor(w_raw[:, WQ, k, :], w_raw[:, WQ, k, :],
                                                              qscale[:, :], ALU.mult), s_pool)
        sp.wait(T["fill"])
        for s in range(NS):
            T["scratch"] = load(xs_rows[:, s, :], filler_row[:, :], s_fill)

        def split_weight(n, hi_lane, lo_lane, need):
            hi_lane.wait(need)
            if hi_lane is act:
                T["whi", n] = act.run(lambda e: e.activation(w_hi[:, n, :, :], w_raw[:, n, :, :], ACT.Copy), s_whi)
            else:
                T["whi", n] = pool.run(lambda e: e.tensor_copy(w_hi[:, n, :, :], w_raw[:, n, :, :]), s_pool)
            lo_lane.wait(T["whi", n], need)
            sig = s_wlo if lo_lane is dve else s_pool
            T["wlo", n] = lo_lane.run(lambda e: e.tensor_tensor(
                w_lo[:, n, :, :], w_raw[:, n, :, :], w_hi[:, n, :, :].bitcast(F32), ALU.subtract), sig)

        side_banks = banks[6:8]
        side = {"n": 0, "free": [[], []], "job": None, "left": [], "bank": 0, "after": [], "later": deque()}
        queue = deque()

        def flush():
            for job, bank, done in side["after"]:
                side["free"][bank] = job["read"](side_banks[bank], done)
                side["later"].extend(job.get("later", []))
            side["after"] = []

        def flush_later(n=None):
            while side["later"] and (n is None or n > 0):
                side["later"].popleft()()
                n = None if n is None else n - 1

        def ticket(*key):
            key = key if len(key) > 1 else key[0]
            if key not in T:
                flush()
            if key not in T:
                flush_later()
            return T[key]

        def side_work(budget):
            while budget > 0 and (side["left"] or queue):
                if not side["left"]:
                    job = queue.popleft()
                    bank = side["n"] % 2
                    side["n"] += 1
                    if any(b == bank for _, b, _ in side["after"]):
                        flush()
                    pe.wait(*side["free"][bank])
                    pe.wait(*[ticket(*k) for k in job["need"]])
                    side.update(job=job, bank=bank, left=list(job["matmuls"]))
                cost, make = side["left"].pop(0)
                bank = side["bank"]
                last = not side["left"]
                done = pe.run(lambda e, m=make, t=side_banks[bank]: m(e, t), s_side if last else None)
                budget -= cost
                if last:
                    T[side["job"]["name"]] = done
                    side["after"].append((side["job"], bank, done))

        def queued_cost():
            return sum(c for c, _ in side["left"]) + sum(c for j in queue for c, _ in j["matmuls"])

        def transposes(src):
            return [(53, lambda e, t, j=j: e.transpose(t[:, j * P:(j + 1) * P], src(j), ident[:, :]))
                    for j in range(4)]

        def hi_lo_products(st_hi, st_lo, mv_hi, mv_lo, ns):
            steps = [(a, b, k) for k in range(KT) for a, b in ((st_hi, mv_hi), (st_lo, mv_hi), (st_hi, mv_lo))]
            return [(ns, lambda e, t, a=a, b=b, k=k, n=n: e.matmul(t[:, :], a(k), b(k), start=(n == 0),
                                                                   stop=(n == len(steps) - 1)))
                    for n, (a, b, k) in enumerate(steps)]

        def split_read(hi, lo, key, hi_wait, lo_wait):
            def read(bank, done):
                act.wait(done, *hi_wait())
                T[key + ("hi",)] = a = act.run(lambda e: e.activation(hi, bank[:, :], ACT.Copy), s_side_act)
                dve.wait(a, *lo_wait())
                T[key + ("lo",)] = b = dve.run(lambda e: e.tensor_tensor(lo, bank[:, :], hi.bitcast(F32),
                                                                         ALU.subtract), s_side_dve)
                return [a, b]
            return read

        def xT_job(b, k):
            free = (lambda: [T["VT", b * GPB - 1]]) if b else (lambda: [])
            return {"name": ("xT", b, k), "need": [("x", b), ("const",)],
                    "matmuls": transposes(lambda j: x_tok[:, b % 2, j, k * P:(k + 1) * P]),
                    "read": split_read(xT_hi[:, k, :], xT_lo[:, k, :], ("xT", b, k), free, free)}

        def project_job(kind, g):
            b, m = divmod(g, GPB)
            n = {"K": WK, "Q": WQ, "VT": WV}[kind]
            cols = slice(m * P, (m + 1) * P)
            bias = bias_col[:, n, m:m + 1]

            def read(bank, done):
                if kind == "VT":
                    act.wait(done, *([T["V", g - 1]] if g else []))
                    T["vT", g] = a = act.run(lambda e: e.activation(vT[:, :], bank[:, :], ACT.Identity, bias=bias),
                                             s_side_act)
                    return [a]
                hi, lo = qk_hi[:, g % 2, n, :], qk_lo[:, g % 2, n, :]
                free = [T["scores", g - 2]] if g >= 2 else []
                act.wait(done, *free)
                a = act.run(lambda e: e.activation(hi, bank[:, :], ACT.Identity, bias=bias), s_side_act)
                dve.wait(a, *free)
                T[kind, g, "lo"] = d = dve.run(lambda e: e.scalar_tensor_tensor(
                    lo, bank[:, :], bias, hi.bitcast(F32), ALU.add, ALU.subtract), s_side_dve)
                return [a, d]

            return {"name": (kind, g),
                    "need": [("whi", n), ("wlo", n), ("bq",)] + [("xT", b, k, p) for k in range(KT) for p in ("hi", "lo")],
                    "matmuls": hi_lo_products(lambda k: w_hi[:, n, k, cols], lambda k: w_lo[:, n, k, cols],
                                              lambda k: xT_hi[:, k, :], lambda k: xT_lo[:, k, :], 213),
                    "read": read}

        def v_job(g):
            def read(bank, done):
                src = bank[:, :].rearrange("p (j h d) -> p j h d", j=QT, h=GH)
                hi, lo = v[:, g % 2, :, :, 0:HD], v[:, g % 2, :, :, HD:2 * HD]
                free = [T["pv_group", g - 2]] if g >= 2 else []
                act.wait(done, *free)
                a = act.run(lambda e: e.activation(hi, src, ACT.Copy), s_side_act)
                dve.wait(a, *free)
                T["v", g] = d = dve.run(lambda e: e.tensor_tensor(lo, src, hi.bitcast(F32), ALU.subtract), s_side_dve)
                return [a, d]
            return {"name": ("V", g), "need": [("vT", g)],
                    "matmuls": transposes(lambda j: vT[:, j * P:(j + 1) * P]), "read": read}

        def oT_job(t):
            b, i = divmod(t, QT)
            free = (lambda: [T["OP", t - 1]]) if t else (lambda: [])
            return {"name": ("OT", t), "need": [("o", (b + 1) * NH - 1)],
                    "matmuls": transposes(lambda k: o_tok[:, b % 2, i, k * P:(k + 1) * P]),
                    "read": split_read(oT_hi[:, :, :].rearrange("p k n -> p (k n)"),
                                       oT_lo[:, :, :].rearrange("p k n -> p (k n)"), ("OT", t), free, free)}

        def layer_norm(src, dst, slot, sig, free=()):
            def moments():
                dve.wait(T["ln_in", slot])
                a = dve.run(lambda e: e.bn_stats(stats[:, slot % 2, :], src), sig)
                dve.wait(a)
                a = dve.run(lambda e: e.bn_aggr(mv[:, slot % 2, :], stats[:, slot % 2, :]), sig)
                pool.wait(a)
                a = pool.run(lambda e: e.tensor_scalar(rstd[:, slot % 2, 0:1], mv[:, slot % 2, 1:2], EPS, None,
                                                       ALU.add), s_side_pool)
                pool.wait(a, T["mhalf"])
                T["rstd", slot] = pool.run(lambda e: e.tensor_tensor(rstd[:, slot % 2, 1:2], rstd[:, slot % 2, 0:1],
                                                                     mhalf[:, :], ALU.pow), s_side_pool)

            def normalise():
                dve.wait(T["rstd", slot], *free)
                T["ln", slot] = dve.run(lambda e: e.tensor_scalar(
                    dst, src, mv[:, slot % 2, 0:1], rstd[:, slot % 2, 1:2], ALU.subtract, ALU.mult), sig)
            return moments, normalise

        T["mhalf"] = T["zero"]

        def o_project_job(t):
            b, i = divmod(t, QT)

            def read(bank, done):
                dve.wait(done, T["x+bo", b], *([T["ln", t - 1]] if t else []))
                T["ln_in", t] = T["res", t] = a = dve.run(lambda e: e.tensor_tensor(
                    res[:, :], bank[:, :], x_tok[:, b % 2, i, :], ALU.add), s_side_dve)
                return [a]

            moments, normalise = layer_norm(res[:, :], x1[:, t, 0:D], t, s_side_dve,
                                            [T["wlo", n] for n in range(4)])
            return {"name": ("OP", t), "need": [("OT", t, "hi"), ("OT", t, "lo"), ("whi", WO), ("wlo", WO)],
                    "matmuls": hi_lo_products(lambda k: oT_hi[:, k, :], lambda k: oT_lo[:, k, :],
                                              lambda k: w_hi[:, WO, k, :], lambda k: w_lo[:, WO, k, :], 213),
                    "read": read, "later": [moments, normalise]}

        def x1T_job(t):
            def read(bank, done):
                act.wait(done, *([T["logit", t - 1]] if t else []))
                T["x1T", t] = a = act.run(lambda e: e.activation(x1T[:, :, :].rearrange("p k n -> p (k n)"),
                                                                 bank[:, :], ACT.Copy), s_side_act)
                return [a]
            return {"name": ("x1t", t), "need": [("ln", t)],
                    "matmuls": transposes(lambda k: x1[:, t, k * P:(k + 1) * P]), "read": read}

        def logit_job(t):
            def read(bank, done):
                dve.wait(done)
                T["logits", t] = a = dve.run(lambda e: e.tensor_tensor(logits[:, t, :], bank[:, 0:NE], br_row[:, :],
                                                                       ALU.add), s_side_dve)
                return [a]
            return {"name": ("logit", t), "need": [("x1T", t)],
                    "matmuls": [(107, lambda e, bank, k=k: e.matmul(bank[:, 0:NE], x1T[:, k, :], wr[:, k, :],
                                                                    start=(k == 0), stop=(k == KT - 1)))
                                for k in range(KT)], "read": read}

        UNIT_TILES = ((3,), (0, 1), (2,))
        units = [(g, h, tiles) for g in range(NG) for h in range(GH) for tiles in UNIT_TILES]
        per_head = len(UNIT_TILES)

        def spans(tiles):
            at = 0
            for i in tiles:
                yield i, at, (i + 1) * P
                at += (i + 1) * P

        def unit_scores(u):
            g, h, tiles = units[u]
            rows = slice(h * HD, (h + 1) * HD)
            bank = banks[u % 2]
            pe.wait(ticket("Q", g, "lo"), ticket("K", g, "lo"))
            if u >= 2:
                pe.wait(T["biased", u - 2])
            for i, at, width in spans(tiles):
                for n, (a, c) in enumerate(((qk_hi, qk_hi), (qk_lo, qk_hi), (qk_hi, qk_lo))):
                    T["s", u] = pe.run(lambda e, i=i, at=at, width=width, n=n, a=a, c=c: e.matmul(
                        bank[:, at:at + width], a[rows, g % 2, 1, i * P:(i + 1) * P], c[rows, g % 2, 0, 0:width],
                        start=(n == 0), stop=(n == 2)), s_scores if n == 2 and i == tiles[-1] else None)
            if h == GH - 1 and u % per_head == per_head - 1:
                T["scores", g] = T["s", u]
            dve.wait(T["s", u], T["const2"])
            if u >= 2:
                dve.wait(T["exp", u - 2])
            for i, at, width in spans(tiles):
                T["biased", u] = dve.run(lambda e, i=i, at=at, width=width: e.tensor_tensor_reduce(
                    out=scores[:, u % 2, at:at + width], in0=bank[:, at:at + width], in1=dist[:, SEQ - width:SEQ],
                    scale=-SLOPE[(g % GPB) * GH + h], scalar=3e38, op0=ALU.add, op1=ALU.min,
                    accum_out=neg_max[:, u % 2, i:i + 1]), s_biased)

        def unit_exp(u):
            g, h, tiles = units[u]
            hd = g * GH + h
            act.wait(T["biased", u])
            if u >= 2:
                act.wait(T["pT", u - 2])
            if u % per_head == 0 and hd >= NRS:
                act.wait(T["inv", hd - NRS])
            for i, at, width in spans(tiles):
                T["exp", u] = act.run(lambda e, i=i, at=at, width=width: e.activation(
                    probs[:, u % 2, at:at + width], scores[:, u % 2, at:at + width], ACT.Exp, scale=-1.0,
                    bias=neg_max[:, u % 2, i:i + 1], accum_out=row_sum[:, hd % NRS, i:i + 1]), s_exp)

        def unit_transpose(u):
            blocks = sum(i + 1 for i in units[u][2])
            bank = banks[2 + u % 2]
            pe.wait(T["exp", u])
            if u >= 2:
                pe.wait(T["pThi", u - 2], T["pTlo", u - 2])
            for j in range(blocks):
                T["pT", u] = pe.run(lambda e, j=j: e.transpose(
                    bank[:, j * P:(j + 1) * P], probs[:, u % 2, j * P:(j + 1) * P], ident[:, :]),
                    s_pT if j == blocks - 1 else None)
            hi, lo = pT_hi[:, u % 2, 0:blocks * P], pT_lo[:, u % 2, 0:blocks * P]
            free = [T["pv", u - 2]] if u >= 2 else []
            act.wait(T["pT", u], *free)
            T["pThi", u] = act.run(lambda e: e.activation(hi, bank[:, 0:blocks * P], ACT.Copy), s_pThi)
            dve.wait(T["pThi", u], *free)
            T["pTlo", u] = dve.run(lambda e: e.tensor_tensor(lo, bank[:, 0:blocks * P], hi.bitcast(F32),
                                                             ALU.subtract), s_pTlo)

        def unit_values(u):
            g, h, tiles = units[u]
            hd = g * GH + h
            bank = banks[4 + hd % 2]
            pe.wait(T["pTlo", u], ticket("v", g))
            if u % per_head == 0 and hd >= 2:
                pe.wait(T["pvsum", hd - 2])
            steps = [(i, j, at + j * P, part) for i, at, _ in spans(tiles) for j in range(i + 1)
                     for part in (pT_hi, pT_lo)]
            for n, (i, j, at, part) in enumerate(steps):
                T["pv", u] = pe.run(lambda e, i=i, j=j, at=at, part=part: e.matmul(
                    bank[0:2 * HD, i * P:(i + 1) * P], v[:, g % 2, j, h, :], part[:, u % 2, at:at + P],
                    start=(j == 0 and part is pT_hi), stop=(j == i and part is pT_lo)),
                    s_pv if n == len(steps) - 1 else None)
            if u % per_head == per_head - 1:
                if h == GH - 1:
                    T["pv_group", g] = T["pv", u]
                act.wait(T["pv", u])
                if hd >= 1:
                    act.wait(T["back", hd - 1])
                T["pvT", hd] = act.run(lambda e: e.activation(pvT[:, :], bank[0:2 * HD, :], ACT.Copy), s_pvT)

        def head_values(hd):
            g, h = divmod(hd, GH)
            b, m = divmod(g, GPB)
            bank = banks[4 + hd % 2]
            pe.wait(T["pvT", hd])
            for i in range(QT):
                T["back", hd] = pe.run(lambda e, i=i: e.transpose(
                    bank[:, i * 2 * HD:(i + 1) * 2 * HD], pvT[:, i * P:(i + 1) * P], ident[0:2 * HD, 0:2 * HD]),
                    s_back_tr if i == QT - 1 else None)
            parts = bank[:, 0:QT * 2 * HD].rearrange("p (i s d) -> p i s d", i=QT, s=2)
            act.wait(T["back", hd])
            if hd >= 2:
                act.wait(T["pvsum", hd - 2])
            T["pvhi", hd] = act.run(lambda e: e.activation(pv_hi[:, hd % 2, :, :], parts[:, :, 0, :], ACT.Copy), s_pvhi)
            dve.wait(T["exp", hd * per_head + per_head - 1])
            if hd >= 2:
                dve.wait(T["o", hd - 2])
            T["inv", hd] = dve.run(lambda e: e.reciprocal(row_inv[:, hd % 2, :], row_sum[:, hd % NRS, :]), s_inv)
            dve.wait(T["pvhi", hd])
            T["pvsum", hd] = dve.run(lambda e: e.tensor_tensor(pv_sum[:, hd % 2, :, :], parts[:, :, 1, :],
                                                               pv_hi[:, hd % 2, :, :], ALU.add), s_pvsum)
            pool.wait(T["pvsum", hd], T["inv", hd], T["scratch"])
            if b >= 2:
                pool.wait(*[ticket("OT", (b - 2) * QT + i) for i in range(QT)])
            T["o", hd] = pool.run(lambda e: e.tensor_tensor(
                o_tok[:, b % 2, :, m * P + h * HD:m * P + (h + 1) * HD], pv_sum[:, hd % 2, :, :],
                row_inv[:, hd % 2, :].unsqueeze(2).to_broadcast([P, QT, HD]), ALU.mult), s_o)

        split_weight(WK, act, dve, T["w", WK])
        for k in range(KT):
            queue.append(xT_job(0, k))
        side_work(1e9)
        flush()
        queue.append(project_job("K", 0))
        side_work(1e9)
        split_weight(WQ, act, dve, T["wq"])
        split_weight(WV, act, dve, T["w", WV])
        flush()
        for job in (project_job("Q", 0), project_job("VT", 0)):
            queue.append(job)
        side_work(1e9)
        queue.append(v_job(0))
        side_work(1e9)
        split_weight(WO, pool, pool, T["w", WO])

        def add_bias_to_x(b):
            pool.wait(*[T["xT", b, k] for k in range(KT)])
            for j in range(QT):
                T["x+bo", b] = pool.run(lambda e, j=j: e.tensor_tensor(
                    x_tok[:, b % 2, j, :], x_tok[:, b % 2, j, :], bo_row[:, :], ALU.add), s_side_pool)

        add_bias_to_x(0)

        lazy = deque()
        per_group = len(units) // NG
        for u in range(len(units) + 3):
            if u < len(units):
                g = units[u][0]
                step = u % per_group
                if step == 0:
                    side_work(1e9)
                    if g + 1 < NG:
                        for kind in ("VT", "K", "Q"):
                            queue.append(project_job(kind, g + 1))
                        queue.append(v_job(g + 1))
                        if (g + 2) % GPB == 0 and g + 2 < NG:
                            b = (g + 2) // GPB
                            for k in range(KT):
                                queue.append(xT_job(b, k))
                    if g % GPB == 0 and g:
                        b = g // GPB - 1
                        lazy.extend(range(b * QT, (b + 1) * QT))
                if lazy and step in (2, 6):
                    t = lazy.popleft()
                    queue.extend((oT_job(t), x1T_job(t - 1), o_project_job(t), logit_job(t - 1)) if t
                                 else (oT_job(t), o_project_job(t)))
                unit_scores(u)
            if 2 <= u < len(units) + 2:
                unit_transpose(u - 2)
            if u < len(units):
                unit_exp(u)
            flush()
            flush_later(1)
            if u < len(units):
                side_work(queued_cost() / (per_group - step))
            if u >= 3:
                unit_values(u - 3)
                if u >= 4 + per_head and (u - 4) % per_head == 0:
                    head_values((u - 4) // per_head - 1)
            if u < len(units) and step == per_group - 1:
                if g % GPB == 2 and g // GPB + 1 < NB:
                    b = g // GPB + 1
                    side_work(1e9)
                    flush()
                    add_bias_to_x(b)
                if g % GPB == 1 and g // GPB >= 1 and g // GPB + 1 < NB:
                    b = g // GPB + 1
                    if b >= 2:
                        sp.wait(ticket("res", (b - 2) * QT + QT - 1))
                        T["x", b] = load_x(b)
        head_values(NB * NH - 1)
        lazy.extend(range(NT - QT, NT))
        while lazy:
            t = lazy.popleft()
            queue.extend((oT_job(t), x1T_job(t - 1), o_project_job(t), logit_job(t - 1)))
        queue.extend((x1T_job(NT - 1), logit_job(NT - 1)))
        side_work(1e9)
        flush()
        flush_later()

        def rt(n):
            return route[:, n, :, :]

        def r_op(make, *waits):
            dve.wait(*waits)
            t = dve.run(make, s_route)
            dve.wait(t)
            return t

        EQ, DIFF, EXPD, HOT, FREE_, RANK, TOT, SCAN_A, SCAN_B, POS, TILES, TMP = range(12)
        mx = route[:, FREE_, :, 0]
        T["mx"] = r_op(lambda e: e.tensor_reduce(mx, logits[:, :, :], AX_X, ALU.max), T["logits", NT - 1])
        r_op(lambda e: e.tensor_tensor(rt(EQ), logits[:, :, :], mx.unsqueeze(2).to_broadcast([P, NT, NE]), ALU.is_equal))
        T["diff"] = r_op(lambda e: e.tensor_tensor(rt(DIFF), logits[:, :, :],
                                                   mx.unsqueeze(2).to_broadcast([P, NT, NE]), ALU.subtract))
        act.wait(T["diff"])
        T["expd"] = act.run(lambda e: e.activation(rt(EXPD), rt(DIFF), ACT.Exp), s_side_act)
        taken = route[:, TMP, :, 0]
        r_op(lambda e: e.tensor_copy(route[:, HOT, :, 0], route[:, EQ, :, 0]))
        r_op(lambda e: e.tensor_scalar(taken, route[:, EQ, :, 0], -1.0, 1.0, ALU.mult, ALU.add))
        for j in range(1, NE):
            T["hot"] = r_op(lambda e, j=j: e.tensor_tensor(route[:, HOT, :, j], route[:, EQ, :, j], taken, ALU.mult))
            if j < NE - 1:
                r_op(lambda e, j=j: e.tensor_tensor(taken, taken, route[:, HOT, :, j], ALU.subtract))
        hot = rt(HOT).rearrange("p t e -> p (t e)")
        pe.wait(T["hot"])
        pe.run(lambda e: e.matmul(banks[0][:, 0:NT * NE], before[:, :], hot, start=True, stop=True))
        T["rank"] = pe.run(lambda e: e.matmul(banks[1][:, 0:NT * NE], ones[:, :], hot, start=True, stop=True), s_side)
        bank_te = [banks[n][:, 0:NT * NE].rearrange("p (t e) -> p t e", e=NE) for n in range(2)]
        r_op(lambda e: e.tensor_copy(rt(TOT), bank_te[1]), T["rank"])
        r_op(lambda e: e.tensor_copy(rt(SCAN_A), bank_te[1]))
        src, dst, step = SCAN_A, SCAN_B, 1
        while step < NT:
            r_op(lambda e, s=src, d=dst, n=step: e.tensor_copy(route[:, d, 0:n, :], route[:, s, 0:n, :]))
            r_op(lambda e, s=src, d=dst, n=step: e.tensor_tensor(route[:, d, n:NT, :], route[:, s, n:NT, :],
                                                                 route[:, s, 0:NT - n, :], ALU.add))
            src, dst, step = dst, src, 2 * step
        full = route[:, EQ, :, :].rearrange("p t e -> p (t e)").rearrange("p (e t) -> p e t", e=NE)
        count = route[:, src, NT - 1, :]
        r_op(lambda e: e.tensor_tensor(full, count.unsqueeze(2).to_broadcast([P, NE, NT]),
                                       small[:, C_FULL:C_FULL + NT].unsqueeze(1).to_broadcast([P, NE, NT]), ALU.is_gt))
        ends = route[:, TILES, 0, :]
        r_op(lambda e: e.tensor_reduce(ends, full, AX_X, ALU.add))
        for j in range(1, NE):
            r_op(lambda e, j=j: e.tensor_tensor(ends[:, j:j + 1], ends[:, j:j + 1], ends[:, j - 1:j], ALU.add))
        begins = route[:, TILES, 1, :]
        r_op(lambda e: e.memset(begins[:, 0:1], 0.0))
        r_op(lambda e: e.tensor_scalar(begins[:, 1:NE], ends[:, 0:NE - 1], float(P), None, ALU.mult))
        past = route[:, DIFF, :, :].rearrange("p t e -> p (t e)")[:, 0:NS * (NE - 1)].rearrange("p (s e) -> p s e", e=NE - 1)
        r_op(lambda e: e.tensor_tensor(past, small[:, C_SLOT:C_SLOT + NS].unsqueeze(2).to_broadcast([P, NS, NE - 1]),
                                       ends[:, 0:NE - 1].unsqueeze(1).to_broadcast([P, NS, NE - 1]), ALU.is_ge),
             T["expd"])
        past_sum = route[:, EQ, :, :].rearrange("p t e -> p (t e)")[:, 0:NS]
        r_op(lambda e: e.tensor_reduce(past_sum, past, AX_X, ALU.add))
        T["slot_expert"] = r_op(lambda e: e.tensor_scalar(slot_expert[:, :], past_sum, float(2 * P), None, ALU.mult))
        r_op(lambda e: e.tensor_tensor(rt(POS), rt(src), rt(TOT), ALU.subtract))
        r_op(lambda e: e.tensor_tensor(rt(POS), rt(POS), bank_te[0], ALU.add))
        r_op(lambda e: e.tensor_tensor(rt(POS), rt(POS), begins.unsqueeze(1).to_broadcast([P, NT, NE]), ALU.add))
        r_op(lambda e: e.tensor_tensor(rt(POS), rt(POS), rt(HOT), ALU.mult))
        r_op(lambda e: e.tensor_reduce(route[:, TMP, :, 0], rt(POS), AX_X, ALU.add))
        T["position"] = r_op(lambda e: e.tensor_copy(position[:, :], route[:, TMP, :, 0]))
        r_op(lambda e: e.tensor_reduce(route[:, TMP, :, 1], rt(EXPD), AX_X, ALU.add))
        r_op(lambda e: e.reciprocal(x1[:, :, D], route[:, TMP, :, 1]))
        T["rows_ready"] = r_op(lambda e: e.tensor_copy(x1[:, :, D + 1], small[:, C_TOKEN:C_TOKEN + NT]))
        r_op(lambda e: e.memset(x1[:, :, D + 2:D + 4], 0.0))

        s_scatter = signal("rows_scattered")
        pool.wait(T["position"], (s_route, s_route.value), T["scratch"])
        for t in range(NT):
            T["scattered"] = pool.run(lambda e, t=t: e.indirect_dma_start(
                out=xs_dram, out_offset=bass.IndirectOffsetOnAxis(ap=position[:, t:t + 1].bitcast(U32), axis=0),
                in_=x1[:, t, :], in_offset=None, bounds_check=NS * P - 1, oob_is_err=False), s_scatter, 16)

        p2 = Map(nc, x1_map.at)
        y = p2.put("y", [P, NS, D], F32)
        xsT_hi = p2.put("xsT_hi", [P, NS, KT, P], F32R)
        xsT_lo = p2.put("xsT_lo", [P, NS, KT, P], F32R)
        up_w = [[p2.put(f"up_{part}{k}", [P, NE, 2 * P], F32R) for k in range(KT)] for part in ("hi", "lo")]
        down_w = [p2.put(f"down_{part}", [P, NE, D], F32R) for part in ("hi", "lo")]
        NUPS = 2
        up_raw = p2.put("up_raw", [P, NUPS, KT, 2, P], F32)
        assert p2.at <= nc._sbuf_addr_for_side("right"), p2.at
        p3 = Map(nc, keep.at)
        hT_hi = p3.put("hT_hi", [P, NS, P], F32R)
        hT_lo = p3.put("hT_lo", [P, NS, P], F32R)
        silu = p3.put("silu", [P, 2, 2, P], F32)
        h_tok = p3.put("h_tok", [P, 2, 2, P], F32)
        NDS = 4
        down_raw = p3.put("down_raw", [P, NDS, D], F32)
        assert p3.at <= x1_map.at
        LN_BUFS = 4
        fin = Map(nc, up_raw_at := p2.at - 4 * NUPS * KT * 2 * P)
        out_rows_sb = [fin.put(f"out_row{n}", [P, D], F32) for n in range(LN_BUFS)]
        fin2 = Map(nc, p3.at - 4 * NDS * D)
        xs_back = [fin2.put(f"xs_back{n}", [P, D], F32) for n in range(NDS)]

        s_upraw = [signal(f"up_raw_loaded{n}") for n in range(NUPS)]
        s_downraw = [signal(f"down_raw_loaded{n}") for n in range(NDS)]
        s_rows = [signal(f"rows_loaded{n}") for n in range(5)]
        s_meta = signal("meta_loaded")
        s_token = signal("token_numbers")
        s_upw_lo_pool = signal("up_lo_by_pool")
        s_upw_hi, s_upw_lo = signal("up_hi"), signal("up_lo")
        s_dw_hi, s_dw_lo = signal("down_hi"), signal("down_lo")
        s_xsT, s_xsT_hi, s_xsT_lo = signal("xsT"), signal("xsT_hi_done"), signal("xsT_lo_done")
        s_up, s_silu, s_h, s_hT, s_hThi, s_hTlo = (signal(n) for n in (
            "up_products", "silu_done", "h_done", "hT_done", "hT_hi_done", "hT_lo_done"))
        s_down, s_y = signal("down_products"), signal("y_added")
        s_fin, s_rstd, s_back = signal("final_dve"), signal("final_pool"), [signal(f"xs_back{n}") for n in range(NDS)]
        s_out = [signal(f"out_written{n}") for n in range(LN_BUFS)]

        phase1_done = [T["mx"]]
        route_done = (s_route, s_route.value)

        def load_up(c, e):
            n = (c * NE + e) % NUPS
            sp.wait(*phase1_done, route_done)
            if c * NE + e >= NUPS:
                prev = c * NE + e - NUPS
                sp.wait(T["uphi", prev], T["uplo", prev])
            cols = slice(c * P, (c + 1) * P)
            for half, W in enumerate((Wg, Wu)):
                T["upraw", c * NE + e] = load(up_raw[:, n, :, half, :],
                                              W[e].rearrange("(k p) f -> p k f", p=P)[:, :, cols], s_upraw[n])

        def split_up(c, e):
            n = (c * NE + e) % NUPS
            idx = c * NE + e
            free = [T["up_chunk", c - 1]] if c else []
            for k in range(KT):
                src = up_raw[:, n, k, :, :].rearrange("p g f -> p (g f)")
                act.wait(T["upraw", idx], *free)
                T["uphi", idx] = act.run(lambda e_, k=k, src=src: e_.activation(up_w[0][k][:, e, :], src, ACT.Copy),
                                         s_upw_hi)
                lane, sig = (dve, s_upw_lo) if e == 0 else (pool, s_upw_lo_pool)
                lane.wait(T["uphi", idx], T["upraw", idx], *free)
                T["uplo", idx] = lane.run(lambda e_, k=k, src=src: e_.tensor_tensor(
                    up_w[1][k][:, e, :], src, up_w[0][k][:, e, :].bitcast(F32), ALU.subtract), sig)

        def load_down(c, e):
            idx = c * NE + e
            n = idx % NDS
            sp.wait(*phase1_done, T["scattered"])
            if idx >= NDS:
                sp.wait(T["dhi", idx - NDS], T["dlo", idx - NDS])
            T["draw", idx] = load(down_raw[:, n, :], Wd[e, c * P:(c + 1) * P, :], s_downraw[n])

        def split_down(c, e):
            idx = c * NE + e
            src = down_raw[:, idx % NDS, :]
            free = [T["down_chunk", c - 1]] if c else []
            act.wait(T["draw", idx], *free)
            T["dhi", idx] = act.run(lambda e_: e_.activation(down_w[0][:, e, :], src, ACT.Copy), s_dw_hi)
            dve.wait(T["dhi", idx], T["draw", idx], *free)
            T["dlo", idx] = dve.run(lambda e_: e_.tensor_tensor(down_w[1][:, e, :], src,
                                                                down_w[0][:, e, :].bitcast(F32), ALU.subtract), s_dw_lo)

        act.wait(*phase1_done, route_done)
        pool.wait(*phase1_done)
        pe.wait(*phase1_done)
        for e in range(NUPS):
            load_up(0, e)
        sp.wait(T["scattered"], route_done)
        for n, s0 in enumerate(range(0, NS, 4)):
            s1 = min(s0 + 4, NS)
            T["rows", n] = load(y[:, s0:s1, :], xs_rows[:, s0:s1, 0:D], s_rows[n])
        T["meta"] = load(meta[:, :, :], xs_rows[:, :, D:ROW], s_meta)
        for e in range(NE):
            split_up(0, e)
            if e + NUPS < NE:
                load_up(0, e + NUPS)
        for e in range(NE):
            load_down(0, e)

        def split_rows(s):
            bank = banks[4 + s % 2]
            pe.wait(T["rows", s // 4])
            if s >= 2:
                pe.wait(T["xsTlo", s - 2])
            for k in range(KT):
                T["xsT", s] = pe.run(lambda e, k=k: e.transpose(bank[:, k * P:(k + 1) * P], y[:, s, k * P:(k + 1) * P],
                                                                ident[:, :]), s_xsT if k == KT - 1 else None)
            hi = xsT_hi[:, s, :, :].rearrange("p k n -> p (k n)")
            lo = xsT_lo[:, s, :, :].rearrange("p k n -> p (k n)")
            act.wait(T["xsT", s])
            T["xsThi", s] = act.run(lambda e: e.activation(hi, bank[:, :], ACT.Copy), s_xsT_hi)
            dve.wait(T["xsThi", s])
            T["xsTlo", s] = dve.run(lambda e: e.tensor_tensor(lo, bank[:, :], hi.bitcast(F32), ALU.subtract), s_xsT_lo)

        pairs = [tuple(s for s in (s0, s0 + 1) if s < NS) for s0 in range(0, NS, 2)]
        U_BANKS, T_BANKS, D_BANKS = (0, 1, 7), (2, 3), (4, 5, 6)
        count_u = {"pair": 0, "down": 0}
        registers, at = {}, {}

        def load_offset(eng, s):
            registers[s] = eng.alloc_register(f"slot{s}_expert")
            eng.load(registers[s], slot_expert[0:1, s:s + 1])

        def take_offset(eng, s, times):
            at[0] = eng.snap(registers[s], min_val=0, max_val=(NE - 1) * 2 * P) * times

        def up_pair(c, pr):
            idx = c * len(pairs) + pr
            slots = pairs[pr]
            bank = banks[U_BANKS[idx % 3]]
            if idx >= 3:
                pe.wait(T["h", idx - 3])
            if pr == 0:
                pe.wait(*[T[part, c * NE + e] for e in range(NE) for part in ("uphi", "uplo")])
            for n, s in enumerate(slots):
                if c == 0:
                    split_rows(s)
                    pe.wait(T["xsTlo", s])
                    pe.run(lambda e, s=s: load_offset(e, s))
                pe.run(lambda e, s=s: take_offset(e, s, 1))
                seq = [(a, w, k) for k in range(KT) for a, w in ((xsT_hi, 0), (xsT_lo, 0), (xsT_hi, 1))]
                for q, (a, w, k) in enumerate(seq):
                    last = q == len(seq) - 1
                    T["up", idx] = pe.run(lambda e, s=s, n=n, q=q, a=a, w=w, k=k, last=last: e.matmul(
                        bank[:, n * 2 * P:(n + 1) * 2 * P], a[:, s, k, :],
                        up_w[w][k][:, :, :].rearrange("p a f -> p (a f)")[:, bass.ds(at[0], 2 * P)],
                        start=(q == 0), stop=last), s_up if last and n == len(slots) - 1 else None)
            m = len(slots)
            gu = bank[:, 0:m * 2 * P].rearrange("p (s g f) -> p s g f", s=m, g=2)
            act.wait(T["up", idx])
            if idx >= 2:
                act.wait(T["h", idx - 2])
            T["silu", idx] = act.run(lambda e: e.activation(silu[:, idx % 2, 0:m, :], gu[:, :, 0, :], ACT.Silu), s_silu)
            dve.wait(T["silu", idx])
            if idx >= 2:
                dve.wait(T["hT", idx - 2])
            T["h", idx] = dve.run(lambda e: e.tensor_tensor(h_tok[:, idx % 2, 0:m, :], gu[:, :, 1, :],
                                                            silu[:, idx % 2, 0:m, :], ALU.mult), s_h)

        def transpose_pair(c, pr):
            idx = c * len(pairs) + pr
            slots = pairs[pr]
            m = len(slots)
            bank = banks[T_BANKS[idx % 2]]
            pe.wait(T["h", idx])
            if idx >= 2:
                pe.wait(T["hTlo", idx - 2])
            for n in range(m):
                T["hT", idx] = pe.run(lambda e, n=n: e.transpose(bank[:, n * P:(n + 1) * P], h_tok[:, idx % 2, n, :],
                                                                 ident[:, :]), s_hT if n == m - 1 else None)
            hi = hT_hi[:, slots[0]:slots[0] + m, :].rearrange("p s f -> p (s f)")
            lo = hT_lo[:, slots[0]:slots[0] + m, :].rearrange("p s f -> p (s f)")
            free = [T["down_chunk", c - 1]] if c else []
            act.wait(T["hT", idx], *free)
            T["hThi", idx] = act.run(lambda e: e.activation(hi, bank[:, 0:m * P], ACT.Copy), s_hThi)
            dve.wait(T["hThi", idx], *free)
            T["hTlo", idx] = dve.run(lambda e: e.tensor_tensor(lo, bank[:, 0:m * P], hi.bitcast(F32), ALU.subtract), s_hTlo)

        def down_slot(c, s):
            idx = c * NS + s
            bank = banks[D_BANKS[idx % 3]]
            pe.wait(T["hTlo", c * len(pairs) + s // 2])
            if idx >= 3:
                pe.wait(T["y", idx - 3])
            if s == 0:
                pe.wait(*[T[part, c * NE + e] for e in range(NE) for part in ("dhi", "dlo")])
            pe.run(lambda e: take_offset(e, s, D // (2 * P)))
            for q, (a, w) in enumerate(((hT_hi, 0), (hT_lo, 0), (hT_hi, 1))):
                T["down", idx] = pe.run(lambda e, q=q, a=a, w=w: e.matmul(
                    bank[:, :], a[:, s, :], down_w[w][:, :, :].rearrange("p a f -> p (a f)")[:, bass.ds(at[0], D)],
                    start=(q == 0), stop=(q == 2)), s_down if q == 2 else None)
            dve.wait(T["down", idx])
            if c == 0:
                T["y", idx] = dve.run(lambda e: e.tensor_copy(y[:, s, :], bank[:, :]), s_y)
            else:
                dve.wait(T["y", idx - NS])
                T["y", idx] = dve.run(lambda e: e.tensor_tensor(y[:, s, :], bank[:, :], y[:, s, :], ALU.add), s_y)

        def final_moments(s):
            nb = s % NDS
            sp.wait(*[T["dlo", NC * NE - 1]])
            if s >= NDS:
                sp.wait(T["res2", s - NDS])
            T["back", s] = load(xs_back[nb][:, :], xs_rows[:, s, 0:D], s_back[nb])
            dve.wait(T["back", s], T["y", (NC - 1) * NS + s], T["meta"])
            T["res2", s] = dve.run(lambda e: e.scalar_tensor_tensor(
                y[:, s, :], y[:, s, :], meta[:, s, 0:1], xs_back[nb][:, :], ALU.mult, ALU.add), s_fin)
            T["ln_in", ("f", s)] = T["res2", s]
            dve.wait(T["res2", s])
            if s >= 2:
                dve.wait(T["fln", s - 2])
            a = dve.run(lambda e: e.bn_stats(stats[:, s % 2, :], y[:, s, :]), s_fin)
            dve.wait(a)
            a = dve.run(lambda e: e.bn_aggr(mv[:, s % 2, :], stats[:, s % 2, :]), s_fin)
            pool.wait(a)
            a = pool.run(lambda e: e.tensor_scalar(rstd[:, s % 2, 0:1], mv[:, s % 2, 1:2], EPS, None, ALU.add), s_rstd)
            pool.wait(a)
            T["frstd", s] = pool.run(lambda e: e.tensor_tensor(rstd[:, s % 2, 1:2], rstd[:, s % 2, 0:1],
                                                               mhalf[:, :], ALU.pow), s_rstd)

        def final_store(s):
            n = s % LN_BUFS
            dve.wait(T["frstd", s], T["uplo", NC * NE - 1])
            if s >= LN_BUFS:
                dve.wait(T["stored", s - LN_BUFS])
            T["fln", s] = dve.run(lambda e: e.tensor_scalar(
                out_rows_sb[n][:, :], y[:, s, :], mv[:, s % 2, 0:1], rstd[:, s % 2, 1:2], ALU.subtract, ALU.mult), s_fin)
            pool.wait(T["fln", s], T["token"])
            T["stored", s] = pool.run(lambda e: e.indirect_dma_start(
                out=out_rows, out_offset=bass.IndirectOffsetOnAxis(ap=token[:, s:s + 1].bitcast(U32), axis=0),
                in_=out_rows_sb[n][:, :], in_offset=None, bounds_check=NT * P - 1, oob_is_err=False), s_out[n], 16)

        for c in range(NC):
            for pr in range(len(pairs) + 1):
                if pr < len(pairs):
                    up_pair(c, pr)
                if pr >= 1:
                    transpose_pair(c, pr - 1)
                if c == 0 and pr == 0:
                    dve.wait(T["meta"])
                    T["token"] = dve.run(lambda e: e.tensor_copy(token[:, :], meta[:, :, 1]), s_token)
                if pr < NE:
                    split_down(c, pr)
                    if c + 1 < NC:
                        load_down(c + 1, pr)
                if c + 1 < NC and pr == 4:
                    for e in range(NUPS):
                        load_up(c + 1, e)
            T["up_chunk", c] = T["up", c * len(pairs) + len(pairs) - 1]
            for s in range(NS):
                down_slot(c, s)
                if c + 1 < NC and s % 4 == 0 and s // 4 < NE:
                    e = s // 4
                    split_up(c + 1, e)
                    if e + NUPS < NE:
                        load_up(c + 1, e + NUPS)
                if c == NC - 1:
                    final_moments(s)
                    if s >= 1:
                        final_store(s - 1)
            T["down_chunk", c] = T["down", c * NS + NS - 1]
        final_store(NS - 1)
        pool.wait(*[T["stored", s] for s in range(NS - LN_BUFS, NS)])

        block = ctx.enter_context(nc.Block())
        block.sync(sp.emit)
        block.gpsimd(pool.emit)
        block.scalar(act.emit)
        block.tensor(pe.emit)
        block.vector(dve.emit)


_INS = ["x", "Wq", "bq", "Wk", "bk", "Wv", "bv", "Wo", "bo"]
_FFN = ["Wr", "br", "Wg", "Wu", "Wd"]


def constants():
    p, c = np.arange(P)[:, None], np.arange(SEQ)[None, :]
    dist = np.where(c - (SEQ - P) > p, MASKED, c - (SEQ - 1)).astype(np.float32)
    scale = np.array([1.0 / (math.sqrt(HD) * s) for s in slopes()], np.float32)
    per_col = np.repeat(scale, HD)
    small = np.zeros((P, N_SMALL), np.float32)
    small[:, C_FULL:C_FULL + NT] = np.arange(NT) * P
    small[:, C_SLOT:C_SLOT + NS] = np.arange(NS)
    small[:, C_TOKEN:C_TOKEN + NT] = np.arange(NT)[None, :] * P + p
    small[:, C_QSCALE:C_QSCALE + KT] = per_col.reshape(KT, P).T
    return {
        "c_ident": np.eye(P, dtype=np.float32),
        "c_dist": dist,
        "c_before": (p < np.arange(P)[None, :]).astype(np.float32),
        "c_small": small,
        "c_qscale": np.broadcast_to(per_col, (P, D)).copy(),
    }


def kernel(**inputs):
    import concourse.bacc as _bacc
    from concourse.bass_utils import run_bass_kernel_spmd as _run

    nc = _bacc.Bacc("TRN2", target_bir_lowering=False, num_devices=1)
    arrays, args = {}, []
    named = [(n, inputs[f"L0_attn_{n}"]) for n in _INS] + [(n, inputs[f"L0_ffn_{n}"]) for n in _FFN]
    for name, a in named + list(constants().items()):
        a = np.ascontiguousarray(a)
        arrays[f"in_{name}_dram"] = a
        args.append(nc.dram_tensor(f"in_{name}_dram", a.shape, mybir.dt.from_np(a.dtype), kind="ExternalInput").ap())
    out = nc.dram_tensor("out_dram", (NB, SEQ, D), F32, kind="ExternalOutput").ap()
    build(nc, *args, out)
    r = _run(nc, [arrays], core_ids=[0])
    return r.results[0]["out_dram"]
```

```python
import math
from collections import deque
from contextlib import ExitStack

import numpy as np

import concourse.bass as bass
from concourse import mybir

F32 = mybir.dt.float32
F32R = mybir.dt.float32r
I32 = mybir.dt.int32
U32 = mybir.dt.uint32
ALU = mybir.AluOpType
ACT = mybir.ActivationFunctionType
AX_X = mybir.AxisListType.X

P = 128
NB, SEQ, D = 4, 512, 512
NH = 16
HD = D // NH
GH = P // HD
KT = D // P
QT = SEQ // P
NG = NB * (NH // GH)
GPB = NH // GH
NT = NB * QT
NE, FF = 4, 2048
NS = NT + NE - 1
SW = NS + NS % 2
NC = FF // P
TRASH = 4096
EPS = 1e-5
MASKED = -1e30
NRS = 4

C_FULL, C_SLOT, C_TOKEN = 0, NT, NT + NS
C_QSCALE = C_TOKEN + NT
C_FIRST = C_QSCALE + KT
C_LANE = C_FIRST + SW + 1
N_SMALL = C_LANE + P


class Signal:

    def __init__(self, ctx, nc, name):
        self.sem = ctx.enter_context(nc.semaphore(name))
        self.value = 0


class Lane:

    def __init__(self):
        self.steps = []
        self.waited = {}

    def wait(self, *tickets):
        latest = {}
        for signal, value in tickets:
            latest[signal] = max(value, latest.get(signal, 0))
        for signal, value in latest.items():
            if self.waited.get(signal, 0) < value:
                self.waited[signal] = value
                self.steps.append(lambda eng, s=signal.sem, v=value: eng.wait_ge(s, v))

    def run(self, make, signal=None, by=1):
        if signal is None:
            self.steps.append(make)
            return None
        self.steps.append(lambda eng: make(eng).then_inc(signal.sem, by))
        signal.value += by
        return (signal, signal.value)

    def emit(self, eng):
        for step in self.steps:
            step(eng)


class Map:

    def __init__(self, nc, at):
        self.nc, self.at = nc, (at + 31) // 32 * 32

    def put(self, name, shape, dtype):
        t = self.nc.alloc_sbuf_tensor_at(name, shape, dtype, offset=self.at)
        self.at += (4 * int(np.prod(shape[1:])) + 31) // 32 * 32
        return t


def slopes():
    start = 2 ** (-2 ** (-(math.log2(NH) - 3)))
    return [float(np.float32(start * start ** i)) for i in range(NH)]


def build(nc, x, Wq, bq, Wk, bk, Wv, bv, Wo, bo, Wr, br, Wg, Wu, Wd,
          c_ident, c_dist, c_before, c_small, c_qscale, out):
    SLOPE = slopes()
    x1_dram = nc.dram_tensor("x1_scratch", (NT * P, D), F32, kind="Internal").ap()
    x_rows = x.rearrange("b (t p) d -> b p t d", p=P)
    out_rows = out.rearrange("b t d -> (b t) d")

    with ExitStack() as ctx:
        ctx.enter_context(nc.allow_non_contiguous_dma(reason="small vectors laid across partitions"))

        def signal(name):
            return Signal(ctx, nc, name)

        banks = [ctx.enter_context(nc.psum_tensor(f"bank{i}", [P, 512], F32)) for i in range(8)]
        pe, act, dve, pool, sp = (Lane() for _ in range(5))

        base = nc._sbuf_addr_for_side("left")
        keep = Map(nc, base)
        ident = keep.put("ident", [P, P], F32)
        small = keep.put("small", [P, N_SMALL], F32)
        logits = keep.put("logits", [P, NT, NE], F32)
        slot_expert = keep.put("slot_expert", [P, NS], I32)
        row_token = keep.put("row_token", [P, NS], I32)
        out_token = keep.put("out_token", [P, NS], I32)
        row_weight = keep.put("row_weight", [P, NS], F32)
        route = keep.put("route", [P, 10, NT, NE], F32)
        hot_pad = keep.put("hot_pad", [P, 2 * NT - 1, NE], F32R)
        stats = keep.put("stats", [P, 2, 6], F32)
        mv = keep.put("mv", [P, 2, 2], F32)
        rstd = keep.put("rstd", [P, 2, 2], F32)
        mhalf = keep.put("mhalf", [P, 1], F32)

        end = nc._sbuf_addr_for_side("right")
        top = end // 32 * 32 - 4 * 2 * QT * D
        x_tok = Map(nc, top).put("x_tok", [P, 2, QT, D], F32)
        NUPS, LN_BUFS = 2, 4
        raw_at = top + 4 * QT * D
        up_raw = Map(nc, raw_at).put("up_raw", [P, NUPS, KT, 2, P], F32)
        final = Map(nc, raw_at)
        out_rows_sb = [final.put(f"out_row{n}", [P, D], F32) for n in range(LN_BUFS)]

        p1 = Map(nc, keep.at)
        WK, WQ, WV, WO = range(4)
        w_hi = [p1.put(f"w_hi{n}", [P, KT, D], F32R) for n in range(3)]
        w_lo = [p1.put(f"w_lo{n}", [P, KT, D], F32R) for n in range(3)]
        after_kqv = p1.at
        w_hi.append(p1.put("w_hi3", [P, KT, D], F32R))
        w_lo.append(p1.put("w_lo3", [P, KT, D], F32R))
        dist = p1.put("dist", [P, SEQ], F32)
        late = Map(nc, p1.at)
        lane_hot = late.put("lane_hot", [P, NT, P], F32R)
        inside = late.put("inside", [P, NT, SW + 1], F32)
        placed = late.put("placed", [P, NT, 3, SW], F32R)
        xT_hi = p1.put("xT_hi", [P, KT, SEQ], F32R)
        xT_lo = p1.put("xT_lo", [P, KT, SEQ], F32R)
        qk_hi = p1.put("qk_hi", [P, 2, SEQ], F32R)
        qk_lo = p1.put("qk_lo", [P, 2, SEQ], F32R)
        k_stack = p1.put("k_stack", [3 * HD, GH, SEQ], F32R)
        q_stack = p1.put("q_stack", [3 * HD, GH, SEQ], F32R)
        v = p1.put("v", [P, 2, QT, 2 * GH, 2 * HD], F32R)
        scores = p1.put("scores", [P, 2, SEQ], F32)
        probs = p1.put("probs", [P, 2, SEQ], F32)
        pT_hi = p1.put("pT_hi", [P, 2, SEQ], F32R)
        pT_lo = p1.put("pT_lo", [P, 2, SEQ], F32R)
        pvT = p1.put("pvT", [2 * HD, SEQ], F32)
        bo_row = p1.put("bo_row", [P, D], F32)
        pv_hi = p1.put("pv_hi", [P, 2, QT, HD], F32)
        pv_sum = p1.put("pv_sum", [P, 2, QT, HD], F32)
        bias_col = p1.put("bias_col", [P, 3, GPB], F32)
        wr = p1.put("wr", [P, KT, NE], F32)
        wr_split = p1.put("wr_split", [P, KT, 2, NE], F32R)
        br_row = p1.put("br_row", [P, NE], F32)
        neg_max = p1.put("neg_max", [P, 2, QT], F32)
        row_sum = p1.put("row_sum", [P, NRS, QT], F32)
        row_inv = p1.put("row_inv", [P, 2, QT], F32)
        before_r = p1.put("before_r", [P, P], F32R)
        ones_r = p1.put("ones_r", [P, P], F32R)
        early = Map(nc, p1.at)
        w_raw = early.put("w_raw", [P, 4, KT, D], F32)
        qscale = early.put("qscale", [P, D], F32)
        before = early.put("before", [P, P], F32)
        ones = early.put("ones", [P, P], F32)
        o_tok = p1.put("o_tok", [P, 2, QT, D], F32)
        oT_hi = p1.put("oT_hi", [P, 2, KT, P], F32R)
        oT_lo = p1.put("oT_lo", [P, 2, KT, P], F32R)
        NX = 2
        x1 = p1.put("x1", [P, NX, D], F32)
        res = p1.put("res", [P, 2, D], F32)
        x1T_hi = p1.put("x1T_hi", [P, 2, KT, P], F32R)
        x1T_lo = p1.put("x1T_lo", [P, 2, KT, P], F32R)
        assert max(p1.at, early.at) <= top, (p1.at, early.at, top)

        s_x = [signal(f"x_loaded{i}") for i in range(2)]
        s_ident = signal("identity_loaded")
        s_const, s_const2 = signal("constants_loaded"), signal("late_constants_loaded")
        s_x1 = [signal(f"x1_written{n}") for n in range(NX)]
        s_pool = signal("pool_setup")
        s_whi, s_wlo = signal("w_hi_done"), signal("w_lo_done")
        s_stack = [signal(f"stacks_loaded{h}") for h in range(GH)]
        s_scores, s_biased, s_exp = signal("scores_done"), signal("biased_done"), signal("exp_done")
        s_pT, s_pThi, s_pTlo = signal("pT_done"), signal("pT_hi_done"), signal("pT_lo_done")
        s_pv, s_pvhi, s_pvsum, s_o = signal("pv_done"), signal("pv_hi_copied"), signal("pv_summed"), signal("o_done")
        s_pvT, s_back_tr = signal("pvT_copied"), signal("values_transposed")
        s_inv = signal("row_inverse_done")
        s_side = signal("side_products_done")
        s_side_act, s_side_dve, s_side_pool = signal("side_act"), signal("side_dve"), signal("side_pool")
        s_route = signal("route_dve")

        T = {}

        def load(dst, src, sig, lane=sp):
            return lane.run(lambda e: e.dma_start(dst, src), sig, 16)

        def load_x(b):
            return load(x_tok[:, (b + 1) % 2, :, :], x_rows[b], s_x[b % 2])

        FIRST = {WK: P, WQ: P, WV: 2 * P, WO: D}
        weights = {WK: Wk, WQ: Wq, WV: Wv, WO: Wo}

        def columns(n, part):
            return slice(FIRST[n], D) if part else slice(0, FIRST[n])

        def part_of(n, cols):
            return 0 if cols.stop <= FIRST[n] else 1

        def load_weight(n, part):
            cols = columns(n, part)
            T["w", n, part] = load(w_raw[:, n, :, cols], weights[n].rearrange("(k p) n -> p k n", p=P)[:, :, cols],
                                   signal(f"w_loaded{n}{part}"))

        T["ident"] = load(ident[:, :], c_ident, s_ident)
        T["x", 0] = load_x(0)
        for n in (WK, WQ, WV):
            load_weight(n, 0)
        load(small[:, :], c_small, s_const)
        for n, vec in enumerate((bk, bq, bv)):
            load(bias_col[:, n, :], vec.rearrange("(m p) -> p m", p=P), s_const)
        T["const"] = load(qscale[:, :], c_qscale, s_const)
        load_weight(WK, 1)
        load_weight(WQ, 1)
        load(dist[:, :], c_dist, s_const2)
        load(before[:, :], c_before, s_const2)
        load(bo_row[:, :], bo.partition_broadcast(P), s_const2)
        load(br_row[:, :], br.partition_broadcast(P), s_const2)
        T["const2"] = load(wr[:, :, :], Wr.rearrange("(k p) e -> p k e", p=P), s_const2)
        load_weight(WV, 1)
        load_weight(WO, 0)
        T["x", 1] = load_x(1)

        pool.run(lambda e: e.memset(mhalf[:, :], -0.5), s_pool)
        pool.run(lambda e: e.memset(ones[:, :], 1.0), s_pool)
        T["mhalf"] = pool.run(lambda e: e.memset(hot_pad[:, :, :].bitcast(F32), 0.0), s_pool)
        pool.wait(T["const"])
        T["bq"] = pool.run(lambda e: e.tensor_tensor(bias_col[:, 1, :], bias_col[:, 1, :],
                                                     small[:, C_QSCALE:C_QSCALE + KT], ALU.mult), s_pool)
        for part in range(2):
            cols = columns(WQ, part)
            pool.wait(T["w", WQ, part])
            T["wq", part] = pool.run(lambda e, cols=cols: e.tensor_tensor(
                w_raw[:, WQ, :, cols], w_raw[:, WQ, :, cols],
                qscale[:, cols].unsqueeze(1).to_broadcast([P, KT, cols.stop - cols.start]), ALU.mult), s_pool)
        pool.wait(T["const2"])
        T["wr_hi"] = pool.run(lambda e: e.tensor_copy(wr_split[:, :, 0, :], wr[:, :, :]), s_pool)
        pool.wait(T["wr_hi"])
        T["wr"] = pool.run(lambda e: e.tensor_tensor(wr_split[:, :, 1, :], wr[:, :, :],
                                                     wr_split[:, :, 0, :].bitcast(F32), ALU.subtract), s_pool)
        pool.wait(T["mhalf"])
        pool.run(lambda e: e.tensor_copy(before_r[:, :], before[:, :]), s_pool)
        T["counting"] = pool.run(lambda e: e.tensor_copy(ones_r[:, :], ones[:, :]), s_pool)

        def split_weight(n, part, need):
            hi_lane, lo_lane, hi_signal, lo_signal = (pool, pool, s_pool, s_pool) if n == WO else (act, dve, s_whi, s_wlo)
            cols = columns(n, part)
            raw, hi, lo = w_raw[:, n, :, cols], w_hi[n][:, :, cols], w_lo[n][:, :, cols]
            hi_lane.wait(need)
            T["whi", n, part] = hi_lane.run(
                lambda e: e.tensor_copy(hi, raw) if n == WO else e.activation(hi, raw, ACT.Copy), hi_signal)
            lo_lane.wait(T["whi", n, part], need)
            T["wlo", n, part] = lo_lane.run(lambda e: e.tensor_tensor(lo, raw, hi.bitcast(F32), ALU.subtract), lo_signal)

        side_banks = banks[6:8]
        side = {"n": 0, "free": [[], []], "job": None, "left": [], "bank": 0, "after": [], "later": deque()}
        queue = deque()
        ALL = 1e8

        def flush():
            for job, bank, done in side["after"]:
                side["free"][bank] = job["read"](side_banks[bank], done)
                side["later"].extend(job.get("later", []))
            side["after"] = []

        def flush_later(n=None):
            while side["later"] and (n is None or n > 0):
                side["later"].popleft()()
                n = None if n is None else n - 1

        def ticket(*key):
            key = key if len(key) > 1 else key[0]
            if key not in T:
                flush()
            if key not in T:
                flush_later()
            while key not in T:
                side_work(1, True)
                side_work(sum(c for c, _ in side["left"]), True)
                flush()
            return T[key]

        def side_work(budget, now=False):
            while budget > 0 and (side["left"] or queue):
                if not side["left"]:
                    now = now or budget >= ALL
                    if not now and any((k if len(k) > 1 else k[0]) not in T for k in queue[0]["need"]):
                        return
                    bank = side["n"] % len(side_banks)
                    if not now and any(b == bank for _, b, _ in side["after"]):
                        return
                    job = queue.popleft()
                    side["n"] += 1
                    if any(b == bank for _, b, _ in side["after"]):
                        flush()
                    pe.wait(*side["free"][bank])
                    pe.wait(*[ticket(*k) for k in job["need"]])
                    side.update(job=job, bank=bank, left=list(job["matmuls"]))
                cost, make = side["left"].pop(0)
                bank = side["bank"]
                last = not side["left"]
                done = pe.run(lambda e, m=make, t=side_banks[bank]: m(e, t), s_side if last else None)
                budget -= cost
                if last:
                    T[side["job"]["name"]] = done
                    side["after"].append((side["job"], bank, done))

        def queued_cost():
            return sum(c for c, _ in side["left"]) + sum(c for j in queue for c, _ in j["matmuls"])

        def transposes(src):
            return [(53, lambda e, t, j=j: e.transpose(t[:, j * P:(j + 1) * P], src(j), ident[:, :]))
                    for j in range(4)]

        def hi_lo_products(st_hi, st_lo, mv_hi, mv_lo, ns, tiles=range(KT)):
            steps = [(a, b, k) for k in tiles for a, b in ((st_hi, mv_hi), (st_lo, mv_hi), (st_hi, mv_lo))]
            return [(ns, lambda e, t, a=a, b=b, k=k, n=n: e.matmul(t[:, :], a(k), b(k), start=(n == 0),
                                                                   stop=(n == len(steps) - 1)))
                    for n, (a, b, k) in enumerate(steps)]

        def split_read(hi, lo, key, hi_wait, lo_wait, n=512):
            def read(bank, done):
                act.wait(done, *hi_wait())
                T[key + ("hi",)] = a = act.run(lambda e: e.activation(hi, bank[:, 0:n], ACT.Copy), s_side_act)
                dve.wait(a, *lo_wait())
                T[key + ("lo",)] = b = dve.run(lambda e: e.tensor_tensor(lo, bank[:, 0:n], hi.bitcast(F32),
                                                                         ALU.subtract), s_side_dve)
                return [b]
            return read

        def xT_job(b, k):
            free = (lambda: [T["K", b * GPB - 1], T["Q", b * GPB - 1], T["V", b * GPB // 2 - 1, 1]]) if b else (lambda: [])
            return {"name": ("xT", b, k), "need": [("x", b), ("ident",)],
                    "matmuls": transposes(lambda j: x_tok[:, (b + 1) % 2, j, k * P:(k + 1) * P]),
                    "read": split_read(xT_hi[:, k, :], xT_lo[:, k, :], ("xT", b, k), free, free)}

        def project_job(kind, g):
            b, m = divmod(g, GPB)
            n = {"K": WK, "Q": WQ}[kind]
            cols = slice(m * P, (m + 1) * P)
            bias = bias_col[:, n, m:m + 1]

            def read(bank, done):
                hi, lo = qk_hi[:, n, :], qk_lo[:, n, :]
                free = [T["stack", g - 1, h] for h in range(GH)] if g else []
                act.wait(done, *free)
                a = act.run(lambda e: e.activation(hi, bank[:, :], ACT.Identity, bias=bias), s_side_act)
                dve.wait(a, *free)
                T[kind, g, "lo"] = d = dve.run(lambda e: e.scalar_tensor_tensor(
                    lo, bank[:, :], bias, hi.bitcast(F32), ALU.add, ALU.subtract), s_side_dve)
                return [d]

            return {"name": (kind, g),
                    "need": [("whi", n, part_of(n, cols)), ("wlo", n, part_of(n, cols)), ("bq",)] + [("xT", b, k, "lo") for k in range(KT)],
                    "matmuls": hi_lo_products(lambda k: w_hi[n][:, k, cols], lambda k: w_lo[n][:, k, cols],
                                              lambda k: xT_hi[:, k, :], lambda k: xT_lo[:, k, :], 213),
                    "read": read}

        def v_job(pair, half):
            heads = slice(pair * 2 * P % D, pair * 2 * P % D + 2 * P)

            def read(bank, done):
                src = bank[:, :].rearrange("p (j h d) -> p j h d", j=2, h=2 * GH)
                j = slice(2 * half, 2 * half + 2)
                hi, lo = v[:, pair % 2, j, :, 0:HD], v[:, pair % 2, j, :, HD:2 * HD]
                free = [T["pv_group", 2 * pair - 3]] if pair >= 2 else []
                act.wait(done, *free)
                a = act.run(lambda e: e.activation(hi, src, ACT.Copy), s_side_act)
                dve.wait(a, *free)
                T["v", pair, half] = d = dve.run(lambda e: e.tensor_tensor(lo, src, hi.bitcast(F32), ALU.subtract),
                                                 s_side_dve)
                return [d]

            matmuls = []
            for n in range(2):
                j = slice((2 * half + n) * P, (2 * half + n + 1) * P)
                for _, make in hi_lo_products(lambda k, j=j: xT_hi[:, k, j], lambda k, j=j: xT_lo[:, k, j],
                                              lambda k: w_hi[WV][:, k, heads], lambda k: w_lo[WV][:, k, heads], 107):
                    matmuls.append((107, lambda e, t, n=n, make=make: make(e, t[:, n * 2 * P:(n + 1) * 2 * P])))
            return {"name": ("V", pair, half),
                    "need": [("whi", WV, part_of(WV, heads)), ("wlo", WV, part_of(WV, heads))] + [("xT", pair * 2 // GPB, k, "lo") for k in range(KT)],
                    "matmuls": matmuls, "read": read}

        def bias_job():
            def read(bank, done):
                dve.wait(done, T["const2"])
                T["bo"] = a = dve.run(lambda e: e.tensor_tensor(bo_row[:, :], bank[:, :], bo_row[:, :], ALU.add),
                                      s_side_dve)
                return [a]
            return {"name": ("bv_wo",), "need": [("bv",), ("whi", WO, 0), ("wlo", WO, 0)],
                    "matmuls": hi_lo_products(lambda k: oT_hi[:, 0, k, :], lambda k: oT_lo[:, 0, k, :],
                                              lambda k: w_hi[WO][:, k, :], lambda k: w_lo[WO][:, k, :], 213),
                    "read": read}

        DONE = (GPB - 1) * GH

        def oT_job(t):
            b, i = divmod(t, QT)
            last = b == NB - 1
            n = (KT - 1 if last else KT) * P
            free = (lambda: [T["OP", t - 2]]) if t >= 2 else (lambda: [])
            hi = oT_hi[:, t % 2, :, :].rearrange("p k n -> p (k n)")[:, 0:n]
            lo = oT_lo[:, t % 2, :, :].rearrange("p k n -> p (k n)")[:, 0:n]
            return {"name": ("OT", t), "need": [("o", b * NH + (DONE if last else NH) - 1)],
                    "matmuls": transposes(lambda k: o_tok[:, b % 2, i, k * P:(k + 1) * P])[0:n // P],
                    "read": split_read(hi, lo, ("OT", t), free, free, n)}

        def oT_last_job():
            free = lambda: [T["OP", NT - 1], T["OP", NT - 2]]
            return {"name": ("OT_last",), "need": [("o", NB * NH - 1)],
                    "matmuls": transposes(lambda i: o_tok[:, (NB - 1) % 2, i, (KT - 1) * P:KT * P]),
                    "read": split_read(oT_hi[:, 0, :, :].rearrange("p k n -> p (k n)"),
                                       oT_lo[:, 0, :, :].rearrange("p k n -> p (k n)"), ("OT_last",), free, free)}

        def layer_norm(src, dst, slot, sig, free):
            def moments():
                dve.wait(T["ln_in", slot])
                a = dve.run(lambda e: e.bn_stats(stats[:, slot % 2, :], src), sig)
                dve.wait(a)
                a = dve.run(lambda e: e.bn_aggr(mv[:, slot % 2, :], stats[:, slot % 2, :]), sig)
                pool.wait(a)
                a = pool.run(lambda e: e.tensor_scalar(rstd[:, slot % 2, 0:1], mv[:, slot % 2, 1:2], EPS, None,
                                                       ALU.add), s_side_pool)
                pool.wait(a, T["mhalf"])
                T["rstd", slot] = pool.run(lambda e: e.tensor_tensor(rstd[:, slot % 2, 1:2], rstd[:, slot % 2, 0:1],
                                                                     mhalf[:, :], ALU.pow), s_side_pool)

            def normalise():
                dve.wait(T["rstd", slot], *free())
                T["ln", slot] = dve.run(lambda e: e.tensor_scalar(
                    dst, src, mv[:, slot % 2, 0:1], rstd[:, slot % 2, 1:2], ALU.subtract, ALU.mult), sig)
                sp.wait(T["ln", slot])
                T["x1_out", slot] = load(x1_dram[slot * P:(slot + 1) * P, :], dst, s_x1[slot % NX])
            return moments, normalise

        def residual(t):
            b, i = divmod(t, QT)
            return x_tok[:, (b + 1) % 2, i, :]

        def summed(t):
            return residual(t) if t // QT == NB - 1 else res[:, t % 2, :]

        def x1_row(t):
            return residual(t) if t // QT == NB - 1 else x1[:, t % NX, :]

        def o_project_job(t, rest=False):
            b = t // QT
            final = rest or b < NB - 1

            def read(bank, done):
                dve.wait(done, ticket("x+bo", b), *([T["ln", t - 2]] if 2 <= t < NT - QT else []))
                T["res", t] = a = dve.run(lambda e: e.tensor_tensor(summed(t), bank[:, :], residual(t), ALU.add),
                                          s_side_dve)
                if final:
                    T["ln_in", t] = a
                return [a]

            moments, normalise = layer_norm(summed(t), x1_row(t), t, s_side_dve,
                                            lambda: [T["wlo", WO, 0]]
                                            + ([T["x1_out", t - NX], T["x1t", t - NX]] if NX <= t < NT - QT else []))
            if rest:
                n, tiles, need = t % QT, [KT - 1], [("OT_last", "lo")]
                at = lambda part: lambda k: part[:, 0, n, :]
            else:
                tiles = range(KT if final else KT - 1)
                need = [("OT", t, "lo"), ("whi", WO, 0), ("wlo", WO, 0)]
                at = lambda part: lambda k: part[:, t % 2, k, :]
            return {"name": ("OP_rest" if rest else "OP", t), "need": need,
                    "matmuls": hi_lo_products(at(oT_hi), at(oT_lo), lambda k: w_hi[WO][:, k, :],
                                              lambda k: w_lo[WO][:, k, :], 213, tiles),
                    "read": read, "later": [moments, normalise] if final else []}

        def x1T_job(t):
            free = (lambda: [T["logit", t - 2]]) if t >= 2 else (lambda: [])
            return {"name": ("x1t", t), "need": [("ln", t)],
                    "matmuls": transposes(lambda k: x1_row(t)[:, k * P:(k + 1) * P]),
                    "read": split_read(x1T_hi[:, t % 2, :, :].rearrange("p k n -> p (k n)"),
                                       x1T_lo[:, t % 2, :, :].rearrange("p k n -> p (k n)"), ("x1T", t), free, free)}

        def logit_job(t):
            def read(bank, done):
                dve.wait(done)
                a = dve.run(lambda e: e.tensor_tensor(logits[:, t, :], bank[:, 0:NE], br_row[:, :], ALU.add), s_side_dve)
                dve.wait(a)
                T["logits", t] = a = dve.run(lambda e: e.tensor_tensor(logits[:, t, :], bank[:, NE:2 * NE],
                                                                       logits[:, t, :], ALU.add), s_side_dve)
                return [a]
            w2 = wr_split[:, :, :, :].rearrange("p k s e -> p k (s e)")
            steps = [(st, k) for k in range(KT) for st in (x1T_hi, x1T_lo)]
            return {"name": ("logit", t), "need": [("x1T", t, "lo"), ("wr",)],
                    "matmuls": [(107, lambda e, bank, q=q, st=st, k=k: e.matmul(
                        bank[:, 0:2 * NE], st[:, t % 2, k, :], w2[:, k, :], start=(q == 0), stop=(q == len(steps) - 1)))
                                for q, (st, k) in enumerate(steps)], "read": read}

        UNIT_TILES = ((3,), (0, 1), (2,))
        units = [(g, h, tiles) for g in range(NG) for h in range(GH) for tiles in UNIT_TILES]
        per_head = len(UNIT_TILES)

        def spans(tiles):
            at = 0
            for i in tiles:
                yield i, at, (i + 1) * P
                at += (i + 1) * P

        stacks_due = deque((g, h) for g in range(NG) for h in range(GH))

        def load_stacks():
            while stacks_due:
                g, h = stacks_due[0]
                if ("Q", g, "lo") not in T or ("K", g, "lo") not in T or (g and ("scores", g - 1, h) not in T):
                    return
                stacks_due.popleft()
                sp.wait(T["K", g, "lo"], T["Q", g, "lo"], *([T["scores", g - 1, h]] if g else []))
                rows = slice(h * HD, (h + 1) * HD)
                for stack, n, parts in ((k_stack, WK, (qk_hi, qk_hi, qk_lo)), (q_stack, WQ, (qk_hi, qk_lo, qk_hi))):
                    for r, part in enumerate(parts):
                        T["stack", g, h] = load(stack[r * HD:(r + 1) * HD, h, :].bitcast(F32),
                                                   part[rows, n, :].bitcast(F32), s_stack[h])

        def unit_scores(u):
            g, h, tiles = units[u]
            bank = banks[u % 2]
            if ("stack", g, h) not in T:
                ticket("Q", g, "lo")
                load_stacks()
            pe.wait(T["stack", g, h])
            if u >= 2:
                pe.wait(T["biased", u - 2])
            for i, at, width in spans(tiles):
                T["s", u] = pe.run(lambda e, i=i, at=at, width=width: e.matmul(
                    bank[:, at:at + width], q_stack[:, h, i * P:(i + 1) * P], k_stack[:, h, 0:width],
                    start=True, stop=True), s_scores if i == tiles[-1] else None)
            if u % per_head == per_head - 1:
                T["scores", g, h] = T["s", u]
            dve.wait(T["s", u], T["const2"])
            if u >= 2:
                dve.wait(T["exp", u - 2])
            for i, at, width in spans(tiles):
                T["biased", u] = dve.run(lambda e, i=i, at=at, width=width: e.tensor_tensor_reduce(
                    out=scores[:, u % 2, at:at + width], in0=bank[:, at:at + width], in1=dist[:, SEQ - width:SEQ],
                    scale=-SLOPE[(g % GPB) * GH + h], scalar=3e38, op0=ALU.add, op1=ALU.min,
                    accum_out=neg_max[:, u % 2, i:i + 1]), s_biased)

        def unit_exp(u):
            g, h, tiles = units[u]
            hd = g * GH + h
            act.wait(T["biased", u])
            if u >= 2:
                act.wait(T["pT", u - 2])
            if u % per_head == 0 and hd >= NRS:
                act.wait(T["inv", hd - NRS])
            for i, at, width in spans(tiles):
                T["exp", u] = act.run(lambda e, i=i, at=at, width=width: e.activation(
                    probs[:, u % 2, at:at + width], scores[:, u % 2, at:at + width], ACT.Exp, scale=-1.0,
                    bias=neg_max[:, u % 2, i:i + 1], accum_out=row_sum[:, hd % NRS, i:i + 1]), s_exp)

        def unit_transpose(u):
            blocks = sum(i + 1 for i in units[u][2])
            bank = banks[2 + u % 2]
            pe.wait(T["exp", u])
            if u >= 2:
                pe.wait(T["pTlo", u - 2])
            for j in range(blocks):
                T["pT", u] = pe.run(lambda e, j=j: e.transpose(
                    bank[:, j * P:(j + 1) * P], probs[:, u % 2, j * P:(j + 1) * P], ident[:, :]),
                    s_pT if j == blocks - 1 else None)
            hi, lo = pT_hi[:, u % 2, 0:blocks * P], pT_lo[:, u % 2, 0:blocks * P]
            free = [T["pv", u - 2]] if u >= 2 else []
            act.wait(T["pT", u], *free)
            T["pThi", u] = act.run(lambda e: e.activation(hi, bank[:, 0:blocks * P], ACT.Copy), s_pThi)
            dve.wait(T["pThi", u], *free)
            T["pTlo", u] = dve.run(lambda e: e.tensor_tensor(lo, bank[:, 0:blocks * P], hi.bitcast(F32),
                                                             ALU.subtract), s_pTlo)

        def unit_values(u):
            g, h, tiles = units[u]
            hd = g * GH + h
            bank = banks[4 + hd % 2]
            pe.wait(T["pTlo", u], ticket("v", g // 2, 0), ticket("v", g // 2, 1))
            if u % per_head == 0 and hd >= 2:
                pe.wait(T["pvsum", hd - 2])
            steps = [(i, j, at + j * P, part) for i, at, _ in spans(tiles) for j in range(i + 1)
                     for part in (pT_hi, pT_lo)]
            for n, (i, j, at, part) in enumerate(steps):
                T["pv", u] = pe.run(lambda e, i=i, j=j, at=at, part=part: e.matmul(
                    bank[0:2 * HD, i * P:(i + 1) * P], v[:, g // 2 % 2, j, g % 2 * GH + h, :], part[:, u % 2, at:at + P],
                    start=(j == 0 and part is pT_hi), stop=(j == i and part is pT_lo)),
                    s_pv if n == len(steps) - 1 else None)
            if u % per_head == per_head - 1:
                if h == GH - 1:
                    T["pv_group", g] = T["pv", u]
                act.wait(T["pv", u])
                if hd >= 1:
                    act.wait(T["back", hd - 1])
                T["pvT", hd] = act.run(lambda e: e.activation(pvT[:, :], bank[0:2 * HD, :], ACT.Copy), s_pvT)

        def head_values(hd):
            g, h = divmod(hd, GH)
            b, m = divmod(g, GPB)
            bank = banks[4 + hd % 2]
            pe.wait(T["pvT", hd])
            for i in range(QT):
                T["back", hd] = pe.run(lambda e, i=i: e.transpose(
                    bank[:, i * 2 * HD:(i + 1) * 2 * HD], pvT[:, i * P:(i + 1) * P], ident[0:2 * HD, 0:2 * HD]),
                    s_back_tr if i == QT - 1 else None)
            parts = bank[:, 0:QT * 2 * HD].rearrange("p (i s d) -> p i s d", i=QT, s=2)
            act.wait(T["back", hd])
            if hd >= 2:
                act.wait(T["pvsum", hd - 2])
            T["pvhi", hd] = act.run(lambda e: e.activation(pv_hi[:, hd % 2, :, :], parts[:, :, 0, :], ACT.Copy), s_pvhi)
            dve.wait(T["exp", hd * per_head + per_head - 1])
            if hd >= 2:
                dve.wait(T["o", hd - 2])
            T["inv", hd] = dve.run(lambda e: e.reciprocal(row_inv[:, hd % 2, :], row_sum[:, hd % NRS, :]), s_inv)
            dve.wait(T["pvhi", hd])
            T["pvsum", hd] = dve.run(lambda e: e.tensor_tensor(pv_sum[:, hd % 2, :, :], parts[:, :, 1, :],
                                                               pv_hi[:, hd % 2, :, :], ALU.add), s_pvsum)
            pool.wait(T["pvsum", hd], T["inv", hd], *raw_read)
            if b >= 2:
                pool.wait(*[ticket("OT", (b - 2) * QT + i) for i in range(QT)])
            T["o", hd] = pool.run(lambda e: e.tensor_tensor(
                o_tok[:, b % 2, :, m * P + h * HD:m * P + (h + 1) * HD], pv_sum[:, hd % 2, :, :],
                row_inv[:, hd % 2, :].unsqueeze(2).to_broadcast([P, QT, HD]), ALU.mult), s_o)

        p2 = Map(nc, keep.at)
        up_w = [[p2.put(f"up_{part}{k}", [P, NE, 2 * P], F32R) for k in range(KT)] for part in ("hi", "lo")]
        down_w = [p2.put(f"down_{part}", [P, NE, D], F32R) for part in ("hi", "lo")]
        assert p2.at <= after_kqv
        y = p2.put("y", [P, NS, D], F32)
        xsT_hi = p2.put("xsT_hi", [P, NS, KT, P], F32R)
        xsT_lo = p2.put("xsT_lo", [P, NS, KT, P], F32R)
        hT_hi = p2.put("hT_hi", [P, NS, P], F32R)
        hT_lo = p2.put("hT_lo", [P, NS, P], F32R)
        silu = p2.put("silu", [P, 2, 2, P], F32)
        h_tok = p2.put("h_tok", [P, 2, 2, P], F32)
        NDS = 4
        down_raw = p2.put("down_raw", [P, NDS, D], F32)
        assert p2.at <= raw_at, p2.at

        s_upraw = [signal(f"up_raw_loaded{n}") for n in range(NUPS)]
        s_downraw = [signal(f"down_raw_loaded{n}") for n in range(NDS)]
        s_rows = [signal(f"rows_gathered{n}") for n in range((NS + 1) // 2)]
        s_upw_hi, s_upw_lo, s_upw_lo_pool = signal("up_hi"), signal("up_lo"), signal("up_lo_by_pool")
        s_dw_hi, s_dw_lo = signal("down_hi"), signal("down_lo")
        s_xsT, s_xsT_hi, s_xsT_lo = signal("xsT"), signal("xsT_hi_done"), signal("xsT_lo_done")
        s_up, s_silu, s_h, s_hT, s_hThi, s_hTlo = (signal(n) for n in (
            "up_products", "silu_done", "h_done", "hT_done", "hT_hi_done", "hT_lo_done"))
        s_down, s_y = signal("down_products"), signal("y_added")
        s_fin, s_rstd = signal("final_dve"), signal("final_pool")
        s_out = [signal(f"out_written{n}") for n in range(LN_BUFS)]

        def up_split(idx):
            return [T[part, idx] for part in ("uphi", "uplo", "uplo_dve") if (part, idx) in T]

        def load_up(c, e):
            n = (c * NE + e) % NUPS
            if c * NE + e >= NUPS:
                prev = c * NE + e - NUPS
                sp.wait(*up_split(prev))
            cols = slice(c * P, (c + 1) * P)
            for half, W in enumerate((Wg, Wu)):
                T["upraw", c * NE + e] = load(up_raw[:, n, :, half, :],
                                              W[e].rearrange("(k p) f -> p k f", p=P)[:, :, cols], s_upraw[n])

        def split_up(c, e):
            n = (c * NE + e) % NUPS
            idx = c * NE + e
            free = [T["up_chunk", c - 1]] if c else [T["K", NG - 1], T["Q", NG - 1], T["V", NG // 2 - 1, 1]]
            for k in range(KT):
                src = up_raw[:, n, k, :, :].rearrange("p g f -> p (g f)")
                act.wait(T["upraw", idx], *free)
                T["uphi", idx] = act.run(lambda e_, k=k, src=src: e_.activation(up_w[0][k][:, e, :], src, ACT.Copy),
                                         s_upw_hi)
                lane, sig = (dve, s_upw_lo) if c and e == 0 and k == 0 else (pool, s_upw_lo_pool)
                lane.wait(T["uphi", idx], T["upraw", idx], *free)
                T["uplo" if lane is pool else "uplo_dve", idx] = lane.run(lambda e_, k=k, src=src: e_.tensor_tensor(
                    up_w[1][k][:, e, :], src, up_w[0][k][:, e, :].bitcast(F32), ALU.subtract), sig)

        for k in range(KT):
            queue.append(xT_job(0, k))
        side_work(ALL)
        flush()
        for n, need in ((WK, T["w", WK, 0]), (WQ, T["wq", 0])):
            split_weight(n, 0, need)
        queue.append(project_job("K", 0))
        side_work(ALL)
        flush()
        split_weight(WV, 0, T["w", WV, 0])
        queue.append(project_job("Q", 0))
        side_work(ALL)
        flush()
        load_stacks()
        queue.extend((v_job(0, 0), v_job(0, 1)))
        side_work(ALL)
        split_weight(WK, 1, T["w", WK, 1])
        split_weight(WQ, 1, T["wq", 1])
        flush()
        split_weight(WV, 1, T["w", WV, 1])
        split_weight(WO, 0, T["w", WO, 0])
        raw_read = [T["wlo", n, 1] for n in (WK, WQ, WV)] + [T["wlo", WO, 0]]
        pool.wait(T["whi", WV, 1], T["wlo", WV, 1], T["const"])
        bv_cols = bias_col[:, 2, :].unsqueeze(2).to_broadcast([P, KT, P])
        T["bv_hi"] = pool.run(lambda e: e.tensor_copy(oT_hi[:, 0, :, :], bv_cols), s_pool)
        pool.wait(T["bv_hi"])
        T["bv"] = pool.run(lambda e: e.tensor_tensor(oT_lo[:, 0, :, :], bv_cols, oT_hi[:, 0, :, :].bitcast(F32),
                                                     ALU.subtract), s_pool)

        def add_bias_to_x(b):
            pool.wait(ticket("bo"), *[ticket("xT", b, k) for k in range(KT)])
            for j in range(QT):
                T["x+bo", b] = pool.run(lambda e, j=j: e.tensor_tensor(
                    x_tok[:, (b + 1) % 2, j, :], x_tok[:, (b + 1) % 2, j, :], bo_row[:, :], ALU.add), s_side_pool)

        def row_jobs(b, n):
            stages = ((0, oT_job), (1, o_project_job), (3, logit_job), (2, x1T_job))
            return [job(b * QT + n - lag) for lag, job in stages if 0 <= n - lag < QT]

        ROW_STEPS = QT + 3
        ROW_UNITS = ((4, 10), (4, 10), (1, 4, 10), ()), ((1, 6), (1, 6), (1, 6), (1,))
        rows_due = deque()
        per_group = len(units) // NG
        x_due = deque(range(2, NB + 1))
        for u in range(len(units) + 3):
            flush()
            flush_later(1)
            if x_due and ("res", (x_due[0] - 2) * QT + QT - 1) in T:
                b = x_due.popleft()
                sp.wait(T["res", (b - 2) * QT + QT - 1])
                if b < NB:
                    T["x", b] = load_x(b)
                else:
                    for e in range(NUPS):
                        load_up(0, e)
            if u < len(units):
                g = units[u][0]
                step = u % per_group
                b, m = divmod(g, GPB)
                if step == 0:
                    ahead = []
                    if m == GPB - 1 and b + 1 < NB:
                        ahead += [xT_job(b + 1, k) for k in range(KT)]
                    if g == 0:
                        ahead.append(v_job(1, 0))
                    if g + 1 < NG:
                        ahead += [project_job("K", g + 1), project_job("Q", g + 1)]
                    if g == 0:
                        ahead.append(bias_job())
                    if m == GPB - 1 and b + 1 < NB:
                        ahead += [v_job((g + 1) // 2, 0), v_job((g + 1) // 2, 1)]
                    elif m < 2 and g:
                        ahead.append(v_job(b * GPB // 2 + 1, m))
                    ticket("Q", g, "lo")
                    queue.extendleft(reversed(ahead))
                    if g == 1:
                        add_bias_to_x(0)
                    if m == 0 and g:
                        rows_due.extend((b - 1, n) for n in range(ROW_STEPS))
                if g == NG - 1 and step == 5:
                    for t in range(NT - QT, NT):
                        queue.append(oT_job(t))
                        if t > NT - QT:
                            queue.append(o_project_job(t - 1))
                    queue.append(o_project_job(NT - 1))
                if rows_due and step in ROW_UNITS[b == NB - 1][m]:
                    queue.extend(row_jobs(*rows_due.popleft()))
                unit_scores(u)
            if 2 <= u < len(units) + 2:
                unit_transpose(u - 2)
            if u < len(units):
                unit_exp(u)
                if g == NG - 1 and step in (1, 3):
                    e = step // 2
                    split_up(0, e)
                    load_up(0, e + NUPS)
                side_work(queued_cost() / (per_group - step))
            if u >= 3:
                unit_values(u - 3)
                if u >= 4 + per_head and (u - 4) % per_head == 0:
                    head_values((u - 4) // per_head - 1)
            if u < len(units):
                side_work(queued_cost() / (per_group - step))
                if step == per_group - 1 and m == GPB - 1 and b + 1 < NB:
                    add_bias_to_x(b + 1)
                load_stacks()
        head_values(NB * NH - 1)
        side_banks.extend(banks[0:4])
        U = len(units)
        side["free"] += [[T["biased", U - 2 + (U % 2)]], [T["biased", U - 1 - (U % 2)]],
                         [T["pTlo", U - 2 + (U % 2)]], [T["pTlo", U - 1 - (U % 2)]]]

        def run_job(job):
            queue.append(job)
            side_work(ALL)
            flush()

        side_work(ALL)
        flush()
        flush_later()
        run_job(oT_last_job())
        t0 = NT - QT
        moments, rows = [], []
        for t in range(t0, NT):
            run_job(o_project_job(t, True))
            moments.append(side["later"].popleft())
            rows.append(side["later"].popleft())
            moments[-1]()
            if t > t0:
                rows[-2]()
        rows[-1]()
        for e in range(NUPS, NE):
            split_up(0, e)
        for job in (x1T_job(t0), x1T_job(t0 + 1), logit_job(t0), x1T_job(t0 + 2), logit_job(t0 + 1),
                    x1T_job(t0 + 3), logit_job(t0 + 2), logit_job(t0 + 3)):
            run_job(job)

        def rt(n):
            return route[:, n, :, :]

        def r_op(make, *waits):
            dve.wait(*waits)
            t = dve.run(make, s_route)
            dve.wait(t)
            return t

        EQ, DIFF, EXPD, MAX, POS, TILES, TMP, W, FULL, PAST = range(10)
        hot_f = hot_pad[:, NT - 1:2 * NT - 1, :].bitcast(F32)
        mx = route[:, MAX, :, 0]
        T["mx"] = r_op(lambda e: e.tensor_reduce(mx, logits[:, :, :], AX_X, ALU.max), T["logits", NT - 1])
        r_op(lambda e: e.tensor_tensor(rt(EQ), logits[:, :, :], mx.unsqueeze(2).to_broadcast([P, NT, NE]), ALU.is_equal))
        T["diff"] = r_op(lambda e: e.tensor_tensor(rt(DIFF), logits[:, :, :],
                                                   mx.unsqueeze(2).to_broadcast([P, NT, NE]), ALU.subtract))
        act.wait(T["diff"])
        T["expd"] = act.run(lambda e: e.activation(rt(EXPD), rt(DIFF), ACT.Exp), s_side_act)
        taken = route[:, TMP, :, 0]
        r_op(lambda e: e.tensor_copy(hot_pad[:, NT - 1:, 0], route[:, EQ, :, 0]), T["mhalf"])
        r_op(lambda e: e.tensor_scalar(taken, route[:, EQ, :, 0], -1.0, 1.0, ALU.mult, ALU.add))
        for j in range(1, NE):
            T["hot"] = r_op(lambda e, j=j: e.tensor_tensor(hot_pad[:, NT - 1:, j], route[:, EQ, :, j], taken, ALU.mult))
            if j < NE - 1:
                r_op(lambda e, j=j: e.tensor_tensor(taken, taken, hot_f[:, :, j], ALU.subtract))
        pe.wait(T["hot"], T["counting"])
        T["counts"] = pe.run(lambda e: e.matmul(banks[1][:, 0:NT * NE], ones_r[:, :], hot_pad[:, NT - 1:, :].rearrange(
            "p t e -> p (t e)"), start=True, stop=True), s_side)
        for n in range(NT):
            T["rank"] = pe.run(lambda e, n=n: e.matmul(
                banks[0][:, 0:NT * NE], (ones_r if n else before_r)[:, :],
                hot_pad[:, NT - 1 - n:2 * NT - 1 - n, :].rearrange("p t e -> p (t e)"),
                start=(n == 0), stop=(n == NT - 1)), s_side if n == NT - 1 else None)
        weight = route[:, W, :, 0]
        r_op(lambda e: e.tensor_reduce(route[:, W, :, 1], rt(EXPD), AX_X, ALU.add), T["expd"])
        T["gate"] = r_op(lambda e: e.reciprocal(weight, route[:, W, :, 1]))
        rank_te = banks[0][:, 0:NT * NE].rearrange("p (t e) -> p t e", e=NE)
        count = route[:, TMP, 0, :]
        r_op(lambda e: e.tensor_reduce(count, banks[1][:, 0:NT * NE].rearrange("p (t e) -> p e t", e=NE), AX_X, ALU.add),
             T["counts"])
        full = route[:, FULL, :, :].rearrange("p t e -> p (t e)").rearrange("p (e t) -> p e t", e=NE)
        r_op(lambda e: e.tensor_tensor(full, count.unsqueeze(2).to_broadcast([P, NE, NT]),
                                       small[:, C_FULL:C_FULL + NT].unsqueeze(1).to_broadcast([P, NE, NT]), ALU.is_gt))
        ends = route[:, TILES, 0, :]
        r_op(lambda e: e.tensor_reduce(ends, full, AX_X, ALU.add))
        for j in range(1, NE):
            r_op(lambda e, j=j: e.tensor_tensor(ends[:, j:j + 1], ends[:, j:j + 1], ends[:, j - 1:j], ALU.add))
        begins = route[:, TILES, 1, :]
        r_op(lambda e: e.memset(begins[:, 0:1], 0.0))
        r_op(lambda e: e.tensor_scalar(begins[:, 1:NE], ends[:, 0:NE - 1], float(P), None, ALU.mult))
        r_op(lambda e: e.tensor_tensor(rt(POS), rank_te, begins.unsqueeze(1).to_broadcast([P, NT, NE]), ALU.add),
             T["rank"])
        r_op(lambda e: e.tensor_tensor(rt(POS), rt(POS), hot_f, ALU.mult))
        position = route[:, TMP, :, 1]
        r_op(lambda e: e.tensor_reduce(position, rt(POS), AX_X, ALU.add))
        r_op(lambda e: e.tensor_tensor(inside[:, :, :], position.unsqueeze(2).to_broadcast([P, NT, SW + 1]),
                                       small[:, C_FIRST:C_FIRST + SW + 1].unsqueeze(1).to_broadcast([P, NT, SW + 1]),
                                       ALU.is_ge))
        slots_to = route[:, TMP, :, 2]
        r_op(lambda e: e.tensor_reduce(slots_to, inside[:, :, :], AX_X, ALU.add))
        lane_of = route[:, TMP, :, 3]
        r_op(lambda e: e.scalar_tensor_tensor(lane_of, slots_to, -float(P), position, ALU.mult, ALU.add))
        r_op(lambda e: e.tensor_tensor(inside[:, :, 0:SW], inside[:, :, 0:SW], inside[:, :, 1:SW + 1], ALU.subtract))
        T["inside"] = r_op(lambda e: e.tensor_tensor(
            placed[:, :, 0, :], inside[:, :, 0:SW],
            small[:, C_TOKEN:C_TOKEN + NT].unsqueeze(2).to_broadcast([P, NT, SW]), ALU.mult))
        for n in range(QT):
            tiles = slice(n * NB, (n + 1) * NB)
            T["lane_hot", n] = dve.run(lambda e, tiles=tiles: e.tensor_tensor(
                lane_hot[:, tiles, :], small[:, C_LANE:C_LANE + P].unsqueeze(1).to_broadcast([P, NB, P]),
                lane_of[:, tiles].unsqueeze(2).to_broadcast([P, NB, P]), ALU.is_equal), s_route)
        w_cols = weight.unsqueeze(2).to_broadcast([P, NT, SW])
        pool.wait(T["inside"], T["gate"])
        T["w_hi"] = pool.run(lambda e: e.tensor_tensor(placed[:, :, 1, :], inside[:, :, 0:SW], w_cols, ALU.mult),
                             s_side_pool)
        T["w_full"] = pool.run(lambda e: e.tensor_tensor(inside[:, :, 0:SW], inside[:, :, 0:SW], w_cols, ALU.mult),
                               s_side_pool)
        pool.wait(T["w_full"])
        T["placed"] = pool.run(lambda e: e.tensor_tensor(placed[:, :, 2, :], inside[:, :, 0:SW],
                                                         placed[:, :, 1, :].bitcast(F32), ALU.subtract), s_side_pool)
        pe.wait(T["inside"], T["placed"])
        for t in range(NT):
            pe.wait(T["lane_hot", t // NB])
            T["listed"] = pe.run(lambda e, t=t: e.matmul(
                banks[2][:, 0:3 * SW], lane_hot[:, t, :], placed[:, t, :, :].rearrange("p k s -> p (k s)"),
                start=(t == 0), stop=(t == NT - 1)), s_side if t == NT - 1 else None)
        number, found = banks[2][:, 0:NS], route[:, POS, :, :].rearrange("p t e -> p (t e)")[:, 0:NS]
        T["row_token"] = r_op(lambda e: e.tensor_scalar(row_token[:, :], number, -1.0, 0.0, ALU.add, ALU.max),
                              T["listed"])
        past = route[:, PAST, :, :].rearrange("p t e -> p (t e)")[:, 0:NS * (NE - 1)].rearrange("p (s e) -> p s e", e=NE - 1)
        r_op(lambda e: e.tensor_tensor(past, small[:, C_SLOT:C_SLOT + NS].unsqueeze(2).to_broadcast([P, NS, NE - 1]),
                                       ends[:, 0:NE - 1].unsqueeze(1).to_broadcast([P, NS, NE - 1]), ALU.is_ge))
        past_sum = route[:, FULL, :, :].rearrange("p t e -> p (t e)")[:, 0:NS]
        r_op(lambda e: e.tensor_reduce(past_sum, past, AX_X, ALU.add))
        T["slot_expert"] = r_op(lambda e: e.tensor_scalar(slot_expert[:, :], past_sum, float(2 * P), None, ALU.mult))
        r_op(lambda e: e.tensor_copy(row_weight[:, :], banks[2][:, SW:SW + NS]))
        T["weight"] = r_op(lambda e: e.tensor_tensor(row_weight[:, :], row_weight[:, :], banks[2][:, 2 * SW:2 * SW + NS],
                                                     ALU.add))
        r_op(lambda e: e.tensor_scalar(found, number, 0.0, float(TRASH), ALU.is_equal, ALU.mult))
        T["out_token"] = r_op(lambda e: e.scalar_tensor_tensor(out_token[:, :], number, -1.0, found, ALU.add, ALU.add))

        phase1_done = [T["mx"]]
        kqv_done = [T["K", NG - 1], T["Q", NG - 1], T["V", NG // 2 - 1, 1]]

        def load_down(c, e):
            idx = c * NE + e
            n = idx % NDS
            sp.wait(*phase1_done)
            if idx >= NDS:
                sp.wait(T["dhi", idx - NDS], T["dlo", idx - NDS])
            T["draw", idx] = load(down_raw[:, n, :], Wd[e, c * P:(c + 1) * P, :], s_downraw[n])

        def split_down(c, e):
            idx = c * NE + e
            src = down_raw[:, idx % NDS, :]
            free = [T["down_chunk", c - 1]] if c else kqv_done
            act.wait(T["draw", idx], *free)
            T["dhi", idx] = act.run(lambda e_: e_.activation(down_w[0][:, e, :], src, ACT.Copy), s_dw_hi)
            dve.wait(T["dhi", idx], T["draw", idx], *free)
            T["dlo", idx] = dve.run(lambda e_: e_.tensor_tensor(down_w[1][:, e, :], src,
                                                                down_w[0][:, e, :].bitcast(F32), ALU.subtract), s_dw_lo)

        for e in range(NE):
            load_down(0, e)
        pool.wait(*phase1_done, T["row_token"], *[T["x1_out", NT - 1 - n] for n in range(NX)])
        for s in range(NS):
            T["rows", s // 2] = pool.run(lambda e, s=s: e.indirect_dma_start(
                out=y[:, s, :], out_offset=None, in_=x1_dram,
                in_offset=bass.IndirectOffsetOnAxis(ap=row_token[:, s:s + 1].bitcast(U32), axis=0),
                bounds_check=NT * P - 1, oob_is_err=False), s_rows[s // 2], 16)

        def split_rows(s):
            bank = banks[4 + s % 3]
            pe.wait(T["rows", s // 2])
            if s >= 3:
                pe.wait(T["xsTlo", s - 3])
            for k in range(KT):
                T["xsT", s] = pe.run(lambda e, k=k: e.transpose(bank[:, k * P:(k + 1) * P], y[:, s, k * P:(k + 1) * P],
                                                                ident[:, :]), s_xsT if k == KT - 1 else None)
            hi = xsT_hi[:, s, :, :].rearrange("p k n -> p (k n)")
            lo = xsT_lo[:, s, :, :].rearrange("p k n -> p (k n)")
            act.wait(T["xsT", s])
            T["xsThi", s] = act.run(lambda e: e.activation(hi, bank[:, :], ACT.Copy), s_xsT_hi)
            dve.wait(T["xsThi", s])
            T["xsTlo", s] = dve.run(lambda e: e.tensor_tensor(lo, bank[:, :], hi.bitcast(F32), ALU.subtract), s_xsT_lo)

        pairs = [tuple(s for s in (s0, s0 + 1) if s < NS) for s0 in range(0, NS, 2)]
        U_BANKS, T_BANKS, D_BANKS = (0, 1, 7), (2, 3), (4, 5, 6)
        registers, at = {}, {}

        def load_offset(eng, s):
            registers[s] = eng.alloc_register(f"slot{s}_expert")
            eng.load(registers[s], slot_expert[0:1, s:s + 1])

        def take_offset(eng, s, times):
            at[0] = eng.snap(registers[s], min_val=0, max_val=(NE - 1) * 2 * P) * times

        def up_pair(c, pr):
            idx = c * len(pairs) + pr
            slots = pairs[pr]
            bank = banks[U_BANKS[idx % 3]]
            if c == 0:
                for s in (slots if pr == 0 else ()) + (pairs[pr + 1] if pr + 1 < len(pairs) else ()):
                    split_rows(s)
            if idx >= 3:
                pe.wait(T["h", idx - 3])
            if pr == 0:
                pe.wait(*[t for e in range(NE) for t in up_split(c * NE + e)])
            for n, s in enumerate(slots):
                if c == 0:
                    pe.wait(T["xsTlo", s], T["slot_expert"])
                    pe.run(lambda e, s=s: load_offset(e, s))
                pe.run(lambda e, s=s: take_offset(e, s, 1))
                seq = [(a, w, k) for k in range(KT) for a, w in ((xsT_hi, 0), (xsT_lo, 0), (xsT_hi, 1))]
                for q, (a, w, k) in enumerate(seq):
                    last = q == len(seq) - 1
                    T["up", idx] = pe.run(lambda e, s=s, n=n, q=q, a=a, w=w, k=k, last=last: e.matmul(
                        bank[:, n * 2 * P:(n + 1) * 2 * P], a[:, s, k, :],
                        up_w[w][k][:, :, :].rearrange("p a f -> p (a f)")[:, bass.ds(at[0], 2 * P)],
                        start=(q == 0), stop=last), s_up if last and n == len(slots) - 1 else None)
            m = len(slots)
            gu = bank[:, 0:m * 2 * P].rearrange("p (s g f) -> p s g f", s=m, g=2)
            act.wait(T["up", idx])
            if idx >= 2:
                act.wait(T["h", idx - 2])
            T["silu", idx] = act.run(lambda e: e.activation(silu[:, idx % 2, 0:m, :], gu[:, :, 0, :], ACT.Silu), s_silu)
            dve.wait(T["silu", idx])
            if idx >= 2:
                dve.wait(T["hT", idx - 2])
            dve.wait(T["weight"])
            for n, s in enumerate(slots):
                T["h", idx] = dve.run(lambda e, n=n, s=s: e.scalar_tensor_tensor(
                    h_tok[:, idx % 2, n, :], gu[:, n, 1, :], row_weight[:, s:s + 1], silu[:, idx % 2, n, :],
                    ALU.mult, ALU.mult), s_h)

        def transpose_pair(c, pr):
            idx = c * len(pairs) + pr
            slots = pairs[pr]
            m = len(slots)
            bank = banks[T_BANKS[idx % 2]]
            pe.wait(T["h", idx])
            if idx >= 2:
                pe.wait(T["hTlo", idx - 2])
            for n in range(m):
                T["hT", idx] = pe.run(lambda e, n=n: e.transpose(bank[:, n * P:(n + 1) * P], h_tok[:, idx % 2, n, :],
                                                                 ident[:, :]), s_hT if n == m - 1 else None)
            hi = hT_hi[:, slots[0]:slots[0] + m, :].rearrange("p s f -> p (s f)")
            lo = hT_lo[:, slots[0]:slots[0] + m, :].rearrange("p s f -> p (s f)")
            free = [T["down_chunk", c - 1]] if c else []
            act.wait(T["hT", idx], *free)
            T["hThi", idx] = act.run(lambda e: e.activation(hi, bank[:, 0:m * P], ACT.Copy), s_hThi)
            dve.wait(T["hThi", idx], *free)
            T["hTlo", idx] = dve.run(lambda e: e.tensor_tensor(lo, bank[:, 0:m * P], hi.bitcast(F32), ALU.subtract), s_hTlo)

        def down_slot(c, s):
            idx = c * NS + s
            bank = banks[D_BANKS[idx % 3]]
            pe.wait(T["hTlo", c * len(pairs) + s // 2])
            if idx >= 3:
                pe.wait(T["y", idx - 3])
            if s == 0:
                pe.wait(T["dlo", c * NE + NE - 1])
            pe.run(lambda e: take_offset(e, s, D // (2 * P)))
            for q, (a, w) in enumerate(((hT_hi, 0), (hT_lo, 0), (hT_hi, 1))):
                T["down", idx] = pe.run(lambda e, q=q, a=a, w=w: e.matmul(
                    bank[:, :], a[:, s, :], down_w[w][:, :, :].rearrange("p a f -> p (a f)")[:, bass.ds(at[0], D)],
                    start=(q == 0), stop=(q == 2)), s_down if q == 2 else None)
            dve.wait(T["down", idx])
            if c:
                dve.wait(T["y", idx - NS])
            T["y", idx] = dve.run(lambda e: e.tensor_tensor(y[:, s, :], bank[:, :], y[:, s, :], ALU.add), s_y)

        def final_moments(s):
            dve.wait(T["y", (NC - 1) * NS + s])
            if s >= 2:
                dve.wait(T["fln", s - 2])
            a = dve.run(lambda e: e.bn_stats(stats[:, s % 2, :], y[:, s, :]), s_fin)
            dve.wait(a)
            a = dve.run(lambda e: e.bn_aggr(mv[:, s % 2, :], stats[:, s % 2, :]), s_fin)
            pool.wait(a)
            a = pool.run(lambda e: e.tensor_scalar(rstd[:, s % 2, 0:1], mv[:, s % 2, 1:2], EPS, None, ALU.add), s_rstd)
            pool.wait(a)
            T["frstd", s] = pool.run(lambda e: e.tensor_tensor(rstd[:, s % 2, 1:2], rstd[:, s % 2, 0:1],
                                                               mhalf[:, :], ALU.pow), s_rstd)

        def final_store(s):
            n = s % LN_BUFS
            dve.wait(T["frstd", s], *up_split(NC * NE - 2), *up_split(NC * NE - 1))
            if s >= LN_BUFS:
                dve.wait(T["stored", s - LN_BUFS])
            T["fln", s] = dve.run(lambda e: e.tensor_scalar(
                out_rows_sb[n][:, :], y[:, s, :], mv[:, s % 2, 0:1], rstd[:, s % 2, 1:2], ALU.subtract, ALU.mult), s_fin)
            pool.wait(T["fln", s], T["out_token"])
            T["stored", s] = pool.run(lambda e: e.indirect_dma_start(
                out=out_rows, out_offset=bass.IndirectOffsetOnAxis(ap=out_token[:, s:s + 1].bitcast(U32), axis=0),
                in_=out_rows_sb[n][:, :], in_offset=None, bounds_check=NT * P - 1, oob_is_err=False), s_out[n], 16)

        NPAIR = len(pairs)
        for c in range(NC):
            for pr in range(NPAIR):
                up_pair(c, pr)
                if pr >= 1:
                    transpose_pair(c, pr - 1)
                if pr < NE:
                    split_down(c, pr)
                    if c + 1 < NC:
                        load_down(c + 1, pr)
                if c + 1 < NC and pr == 4:
                    for e in range(NUPS):
                        load_up(c + 1, e)
            T["up_chunk", c] = T["up", c * NPAIR + NPAIR - 1]
            for s in range(NS):
                if c + 1 < NC and s % 3 == 0 and s // 3 < NE:
                    e = s // 3
                    split_up(c + 1, e)
                    if e + NUPS < NE:
                        load_up(c + 1, e + NUPS)
                down_slot(c, s)
                if s == 1:
                    transpose_pair(c, NPAIR - 1)
                if c == NC - 1:
                    final_moments(s)
                    if s >= 1:
                        final_store(s - 1)
            T["down_chunk", c] = T["down", c * NS + NS - 1]
        final_store(NS - 1)
        pool.wait(*[T["stored", s] for s in range(NS - LN_BUFS, NS)])

        block = ctx.enter_context(nc.Block())
        block.sync(sp.emit)
        block.gpsimd(pool.emit)
        block.scalar(act.emit)
        block.tensor(pe.emit)
        block.vector(dve.emit)


_INS = ["x", "Wq", "bq", "Wk", "bk", "Wv", "bv", "Wo", "bo"]
_FFN = ["Wr", "br", "Wg", "Wu", "Wd"]


def constants():
    p, c = np.arange(P)[:, None], np.arange(SEQ)[None, :]
    dist = np.where(c - (SEQ - P) > p, MASKED, c - (SEQ - 1)).astype(np.float32)
    scale = np.array([1.0 / (math.sqrt(HD) * s) for s in slopes()], np.float32)
    per_col = np.repeat(scale, HD)
    small = np.zeros((P, N_SMALL), np.float32)
    small[:, C_FULL:C_FULL + NT] = np.arange(NT) * P
    small[:, C_SLOT:C_SLOT + NS] = np.arange(NS)
    small[:, C_TOKEN:C_TOKEN + NT] = np.arange(NT)[None, :] * P + p + 1
    small[:, C_FIRST:C_FIRST + SW + 1] = np.arange(SW + 1) * P
    small[:, C_LANE:C_LANE + P] = np.arange(P) - P
    small[:, C_QSCALE:C_QSCALE + KT] = per_col.reshape(KT, P).T
    return {
        "c_ident": np.eye(P, dtype=np.float32),
        "c_dist": dist,
        "c_before": (p < np.arange(P)[None, :]).astype(np.float32),
        "c_small": small,
        "c_qscale": np.broadcast_to(per_col, (P, D)).copy(),
    }


def kernel(**inputs):
    import concourse.bacc as _bacc
    from concourse.bass_utils import run_bass_kernel_spmd as _run

    nc = _bacc.Bacc("TRN2", target_bir_lowering=False, num_devices=1)
    arrays, args = {}, []
    named = [(n, inputs[f"L0_attn_{n}"]) for n in _INS] + [(n, inputs[f"L0_ffn_{n}"]) for n in _FFN]
    for name, a in named + list(constants().items()):
        a = np.ascontiguousarray(a)
        arrays[f"in_{name}_dram"] = a
        args.append(nc.dram_tensor(f"in_{name}_dram", a.shape, mybir.dt.from_np(a.dtype), kind="ExternalInput").ap())
    out = nc.dram_tensor("out_dram", (NB, SEQ, D), F32, kind="ExternalOutput").ap()
    build(nc, *args, out)
    r = _run(nc, [arrays], core_ids=[0])
    return r.results[0]["out_dram"]
```
